# Optimizing a Trainium2 kernel written in Bass

```python
import numpy as np
import jax
import jax.numpy as jnp

def _softmax(x, axis=-1):
    return jax.nn.softmax(x, axis=axis)

def _gelu(x):
    return jax.nn.gelu(x, approximate=True)

def _silu(x):
    return jax.nn.silu(x)

def _sigmoid(x):
    return jax.nn.sigmoid(x)

def _layernorm(x, axis=-1, eps=1e-05):
    m = jnp.mean(x, axis=axis, keepdims=True)
    v = jnp.var(x, axis=axis, keepdims=True)
    return (x - m) / jnp.sqrt(v + eps)

def _scatter_add(tgt, idx, src, axis=0):
    return tgt.at[idx].add(src)

def _segment_sum(src, seg, n):
    return jax.ops.segment_sum(src, seg, n)
kernel_name = 'mk_conv_preact_d2_conv_nchw64_r2_44e20b'

def setup_inputs(seed: int=0):
    np.random.seed(seed)
    _w = jnp.asarray

    def _rec_inputs():
        import jax
        import jax.numpy as jnp
        _gk = jax.random.key(seed)
        x = -0.0009438 + 1 * jax.random.normal(jax.random.fold_in(_gk, 1), (2, 32, 48, 48), jnp.float32)
        return x
    x = _rec_inputs()

    def _L0_conv_setup():
        import jax, jax.numpy as jnp
        from jax import lax
        import numpy as np
        KSIZE = 3
        SCALE = 2
        SOFTMAX_SCALE = 10.0
        EPS = 0.0001

        def prelu(x, a):
            return jnp.where(x >= 0, x, a * x)

        def conv1x1(x, W, b):
            return jnp.einsum('bchw,oc->bohw', x, W) + b[None, :, None, None]

        def extract_patches(x, k, s):
            B, C, H, W = x.shape
            Ho, Wo = (-(-H // s), -(-W // s))
            ph = max(0, (Ho - 1) * s + k - H)
            pw = max(0, (Wo - 1) * s + k - W)
            xp = jnp.pad(x, ((0, 0), (0, 0), (ph // 2, ph - ph // 2), (pw // 2, pw - pw // 2)))
            sl = [xp[:, :, i:i + s * (Ho - 1) + 1:s, j:j + s * (Wo - 1) + 1:s] for i in range(k) for j in range(k)]
            p = jnp.stack(sl, axis=2).reshape(B, C, k, k, Ho, Wo)
            return p.transpose(0, 4, 5, 1, 2, 3).reshape(B, Ho * Wo, C, k, k)
        key = jax.random.key(seed)
        ks = jax.random.split(key, 8)
        B, C, H, W = (2, 32, 48, 48)
        Cr = C // 2
        return {'x': jax.random.normal(ks[0], (B, C, H, W), jnp.float32), 'W1': jax.random.normal(ks[1], (Cr, C), jnp.float32) * 0.1, 'b1': jnp.zeros((Cr,), jnp.float32), 'a1': jnp.full((1,), 0.25, jnp.float32), 'W2': jax.random.normal(ks[2], (Cr, C), jnp.float32) * 0.1, 'b2': jnp.zeros((Cr,), jnp.float32), 'a2': jnp.full((1,), 0.25, jnp.float32), 'Wa': jax.random.normal(ks[3], (C, C), jnp.float32) * 0.1, 'ba': jnp.zeros((C,), jnp.float32), 'aa': jnp.full((1,), 0.25, jnp.float32), 'Wd': jax.random.normal(ks[4], (C, C, 3, 3), jnp.float32) * 0.05, 'bd': jnp.zeros((C,), jnp.float32)}
    _L0_conv_all = _L0_conv_setup()
    _L0_conv_in = {k: v for k, v in _L0_conv_all.items() if k in ('W1', 'b1', 'a1', 'W2', 'b2', 'a2', 'Wa', 'ba', 'aa', 'Wd', 'bd')}
    del _L0_conv_all

    def _L1_conv_setup():
        import jax, jax.numpy as jnp
        import numpy as np

        def _dct2_matrix(n: int) -> jnp.ndarray:
            k = np.arange(n)[:, None].astype(np.float64)
            m = np.arange(n)[None, :].astype(np.float64)
            d = np.cos(np.pi * (2.0 * m + 1.0) * k / (2.0 * n))
            scale = np.full((n, 1), np.sqrt(2.0 / n))
            scale[0, 0] = np.sqrt(1.0 / n)
            return jnp.asarray((scale * d).astype(np.float32))
        key = jax.random.key(seed)
        x = jax.random.normal(key, (32, 32, 112, 112), dtype=jnp.float32)
        return {'x': x}
    _L1_conv_all = _L1_conv_setup()
    _L1_conv_in = {k: v for k, v in _L1_conv_all.items() if k in ()}
    del _L1_conv_all
    return {'x': x, 'L0_conv_W1': _L0_conv_in['W1'], 'L0_conv_b1': _L0_conv_in['b1'], 'L0_conv_a1': _L0_conv_in['a1'], 'L0_conv_W2': _L0_conv_in['W2'], 'L0_conv_b2': _L0_conv_in['b2'], 'L0_conv_a2': _L0_conv_in['a2'], 'L0_conv_Wa': _L0_conv_in['Wa'], 'L0_conv_ba': _L0_conv_in['ba'], 'L0_conv_aa': _L0_conv_in['aa'], 'L0_conv_Wd': _L0_conv_in['Wd'], 'L0_conv_bd': _L0_conv_in['bd']}

def reference(x, L0_conv_W1, L0_conv_b1, L0_conv_a1, L0_conv_W2, L0_conv_b2, L0_conv_a2, L0_conv_Wa, L0_conv_ba, L0_conv_aa, L0_conv_Wd, L0_conv_bd):
    import jax
    import jax.numpy as jnp

    def _L0_conv_ref(x, W1, b1, a1, W2, b2, a2, Wa, ba, aa, Wd, bd):
        import jax, jax.numpy as jnp
        from jax import lax
        import numpy as np
        KSIZE = 3
        SCALE = 2
        SOFTMAX_SCALE = 10.0
        EPS = 0.0001

        def prelu(x, a):
            return jnp.where(x >= 0, x, a * x)

        def conv1x1(x, W, b):
            return jnp.einsum('bchw,oc->bohw', x, W) + b[None, :, None, None]

        def extract_patches(x, k, s):
            B, C, H, W = x.shape
            Ho, Wo = (-(-H // s), -(-W // s))
            ph = max(0, (Ho - 1) * s + k - H)
            pw = max(0, (Wo - 1) * s + k - W)
            xp = jnp.pad(x, ((0, 0), (0, 0), (ph // 2, ph - ph // 2), (pw // 2, pw - pw // 2)))
            sl = [xp[:, :, i:i + s * (Ho - 1) + 1:s, j:j + s * (Wo - 1) + 1:s] for i in range(k) for j in range(k)]
            p = jnp.stack(sl, axis=2).reshape(B, C, k, k, Ho, Wo)
            return p.transpose(0, 4, 5, 1, 2, 3).reshape(B, Ho * Wo, C, k, k)
        B, C, H, W = x.shape
        s, k = (SCALE, KSIZE)
        kernel = s * k
        embed_w = prelu(conv1x1(x, Wa, ba), aa)
        match_in = prelu(conv1x1(x, W1, b1), a1)
        raw_w = extract_patches(embed_w, kernel, s)
        ref = x.reshape(B, C, H // s, s, W // s, s).mean(axis=(3, 5))
        ref = prelu(conv1x1(ref, W2, b2), a2)
        w = extract_patches(ref, k, 1)
        norm = jnp.maximum(jnp.sqrt(jnp.sum(w * w, axis=(2, 3, 4), keepdims=True)), EPS)
        wn = (w / norm).reshape(B, -1, C // 2 * k * k)
        xp = extract_patches(match_in, k, 1).reshape(B, -1, C // 2 * k * k)
        yi = jnp.einsum('blc,bqc->blq', wn, xp)
        yi = jax.nn.softmax(yi * SOFTMAX_SCALE, axis=1)
        L = H // s * (W // s)
        yi = yi.reshape(B, L, H, W)

        def tconv(y, wk):
            wf = jnp.flip(wk, axis=(-2, -1)).transpose(1, 0, 2, 3)
            pad = kernel - 1 - s
            return lax.conv_general_dilated(y[None], wf, (1, 1), ((pad, pad), (pad, pad)), lhs_dilation=(s, s), dimension_numbers=('NCHW', 'OIHW', 'NCHW'))[0]
        yt = jax.vmap(tconv)(yi, raw_w)
        yd = lax.conv_general_dilated(yt, Wd, (2, 2), ((1, 1), (1, 1)), dimension_numbers=('NCHW', 'OIHW', 'NCHW'))
        yd = yd + bd[None, :, None, None]
        return (yd / 6.0)[:, :, :H, :W]

    def _L1_conv_ref(x):
        import jax, jax.numpy as jnp
        import numpy as np

        def _dct2_matrix(n: int) -> jnp.ndarray:
            k = np.arange(n)[:, None].astype(np.float64)
            m = np.arange(n)[None, :].astype(np.float64)
            d = np.cos(np.pi * (2.0 * m + 1.0) * k / (2.0 * n))
            scale = np.full((n, 1), np.sqrt(2.0 / n))
            scale[0, 0] = np.sqrt(1.0 / n)
            return jnp.asarray((scale * d).astype(np.float32))
        B, C, H, W = x.shape
        Dh = _dct2_matrix(H)
        Dw = _dct2_matrix(W)
        y = jnp.einsum('kh,bchw->bckw', Dh, x)
        y = jnp.einsum('lw,bckw->bckl', Dw, y)
        return y

    def _gn(v, G=32, eps=1e-05):
        B_, C_, H_, W_ = v.shape
        g = v.reshape(B_, G, C_ // G, H_, W_)
        m = jnp.mean(g, axis=(2, 3, 4), keepdims=True)
        s = jnp.var(g, axis=(2, 3, 4), keepdims=True)
        return ((g - m) / jnp.sqrt(s + eps)).reshape(v.shape)

    def _ln_c(v, eps=1e-06):
        m = jnp.mean(v, axis=1, keepdims=True)
        s = jnp.var(v, axis=1, keepdims=True)
        return (v - m) / jnp.sqrt(s + eps)

    def _ln_t(v, eps=1e-05):
        m = jnp.mean(v, axis=-1, keepdims=True)
        s = jnp.var(v, axis=-1, keepdims=True)
        return (v - m) / jnp.sqrt(s + eps)

    def _to_tokens(v):
        B_, C_, H_, W_ = v.shape
        return v.reshape(B_, C_, H_ * W_).transpose(0, 2, 1)

    def _from_tokens(t, like):
        B_, C_, H_, W_ = like.shape
        return t.transpose(0, 2, 1).reshape(B_, C_, H_, W_)
    x = x + _L0_conv_ref(_gn(x), L0_conv_W1, L0_conv_b1, L0_conv_a1, L0_conv_W2, L0_conv_b2, L0_conv_a2, L0_conv_Wa, L0_conv_ba, L0_conv_aa, L0_conv_Wd, L0_conv_bd)
    x = x + _L1_conv_ref(_gn(x))
    return x

_drawn_inputs = setup_inputs


def setup_inputs(seed=0):
    import zlib

    import numpy as np

    out = dict(_drawn_inputs(seed))
    spreads = {'L0_conv_b1': (0.0, 0.1),
     'L0_conv_b2': (0.0, 0.1),
     'L0_conv_ba': (0.0, 0.1),
     'L0_conv_bd': (0.0, 0.59)}
    factors = {}
    for name, (base, spread) in spreads.items():
        noise = np.random.default_rng([zlib.crc32(name.encode()), seed]).standard_normal(out[name].shape)
        drawn = base * np.exp(spread * noise) if base else spread * noise
        out[name] = jnp.asarray(drawn.astype(out[name].dtype))
    for name, factor in factors.items():
        out[name] = (out[name] * factor).astype(out[name].dtype)
    return out
```

```python
from contextlib import ExitStack

import concourse.bass as bass
import concourse.mybir as mybir
import numpy as np

F32 = mybir.dt.float32
F32R = mybir.dt.float32r
ALU = mybir.AluOpType
ACT = mybir.ActivationFunctionType
AX = mybir.AxisListType

B, C, H, W = 2, 32, 48, 48
CR = C // 2
Q = H * W
HL, WL = H // 2, W // 2
L = HL * WL
HALF = L // 2
ROWS = 8
CHUNK = ROWS * W
NCH = Q // CHUNK
TPC = CHUNK // 128
NT = B * Q // 128
NG = B * NCH
LT = L // 128
LREM = L - 128 * LT
PADC = 2 * W
WIN = PADC + CHUNK + W
NDJ = 4
MY = HL + 2
VROW = MY * WL
VHALF = VROW // 2
EW = W + 4
GN_EPS = 1e-5
NORM_EPS = 1e-4
SOFTMAX_SCALE = 10.0
LAG = 4

NK = 4 * LT + 2 + LT + 1
PAIR, TOP = 4 * LT, 4 * LT + 2
ALPHA, FULL, BETA = 0, 1, 2
TAP_SRC = [(ALPHA, 2 * WL), (FULL, WL), (FULL, 0), (BETA, 0)]

P_W1, P_W2, P_WA, P_WD = 0, 96, 192, 288
P_B1, P_B2, P_BA, P_A1, P_A2, P_AA, P_BD = 576, 577, 578, 579, 580, 581, 582
NP = 584

UNITS = [(dy, dx) for dy in (-1, 0, 1) for dx in (-1, 0, 1)]
VARIANT = {0: 0, -1: 1, 1: 2}


def misc_plan():
    plan = []
    for b in range(B):
        plan += [("conv2", b, i, "act") for i in range(2)]
        plan += [("conv1", b, i, "act") for i in range(NCH)]
        plan += [("conva", b, i, "act") for i in range(NCH)]
        plan += [("norm", b, i, "act") for i in range(2)]
        plan += [("u", b, i, "act") for i in range(8)]
        plan += [("k", b, i, "dve") for i in range(7)]
        plan += [("kc", b, i, "dve") for i in range(3)]
    for b in range(B):
        plan += [("cc", b, 0, "dve")]
        plan += [("zn", b, i, "act") for i in range(3)]
        plan += [("xt", b, i, "dve") for i in range(3)]
        plan += [("d1", b, i, "act") for i in range(4)]
        plan += [("d2", b, i, "dve") for i in range(4)]
    return plan


def conv_no(name, b, i):
    return (2 + 2 * NCH) * b + {"conv2": 0, "conv1": 2, "conva": 2 + NCH}[name] + i


def embed_splits(k):
    b, i = k // (2 + 2 * NCH), k % (2 + 2 * NCH) - (2 + NCH)
    return NCH * b + i + 1 if i >= 0 else 0


def column_copies(g):
    return 6 * (g + 1) + 4 * (g // NCH + 1)


def grouped(bank, blocks, size):
    return bank[:, 0:size * len(blocks)].rearrange("p (n c) -> p n c", c=size)


PREP_STEP, CONV_STEP, CONVA_STEP, NORM_STEP, SUMS_STEP, TAPS_STEP, COL_STEP, COS_STEP = 2, 3, 5, 7, 9, 15, 22, 25

K_GROUPS = [range(4 * n, 4 * n + 4) for n in range(4)] + [range(PAIR, TOP), range(TOP, TOP + 4), range(TOP + 4, NK)]
KC_GROUPS = [range(0, PAIR), range(PAIR, TOP), range(TOP, NK)]


def program(nc, x, params, dct, out):
    plan = misc_plan()
    misc_no = {(name, b, i): n for n, (name, b, i, _) in enumerate(plan)}

    def emptied(n):
        eng = plan[n][3]
        return eng, sum(p[3] == eng for p in plan[:n + 1])

    with ExitStack() as ctx:
        def sb(name, shape, dt=F32):
            return ctx.enter_context(nc.sbuf_tensor(name, shape, dt))

        def pb(name, shape):
            return ctx.enter_context(nc.psum_tensor(name, shape, F32))

        def sem(name):
            return ctx.enter_context(nc.semaphore(name))

        def sems(name, n=B):
            return [sem(f"{name}{i}") for i in range(n)]

        ident = sb("ident", [128, 128])
        ones = sb("ones", [128, 128])
        par = sb("par", [128, NP])
        wst = sb("wst", [96, P_WD], F32R)
        cosm = sb("cosm", [W, W])
        bd6 = sb("bd6", [128, 1])
        bnst = sb("bnst", [96, NCH, 6])
        bnst2 = sb("bnst2", [128, NCH, 6])
        mv2 = sb("mv2", [128, 4])
        mv = sb("mv", [96, 4])
        y = sb("y", [128, 2, 2, LT + 1, WIN], F32R)
        ycol = sb("ycol", [128, B, 2, LT + 1, H + 6], F32R)
        kh = [sb("kh0", [128, NK, 128], F32R)]
        kl = [sb("kl0", [128, NK, 128], F32R)]
        kch = [sb(f"kch{b}", [128, NK, C], F32R) for b in range(B)]
        kcl = [sb(f"kcl{b}", [128, NK, C], F32R) for b in range(B)]
        vim = sb("vim", [128, Q])
        v2 = sb("v2", [128, Q])
        p = sb("p", [128, 2, L])
        mh = sb("mh", [128, 2, CHUNK], F32R)
        ml = sb("ml", [128, 2, CHUNK], F32R)
        mr = sb("mr", [48, 2, CHUNK], F32R)
        wh = [sb(f"wh{b}", [128, L], F32R) for b in range(B)]
        wl = [sb(f"wl{b}", [128, L], F32R) for b in range(B)]
        wr = [sb(f"wr{b}", [48, L], F32R) for b in range(B)]
        negm = sb("negm", [128, 2])
        psm = sb("psm", [128, 2])
        rps = sb("rps", [128, 2])
        z = sb("z", [96, 2, CHUNK])
        zneg = sb("zneg", [96, CHUNK])
        with ExitStack() as over:
            kh.append(over.enter_context(nc.sbuf_tensor("kh1", [128, NK, 128], F32R)))
            kl.append(over.enter_context(nc.sbuf_tensor("kl1", [128, NK, 128], F32R)))
        with ExitStack() as over:
            xn = over.enter_context(nc.sbuf_tensor("xn", [96, Q], F32))
        e3 = sb("e3", [96, EW * EW], F32R)
        x3 = sb("x3", [96, Q], F32R)
        mimg = sb("mimg", [96, Q + 2 * (W + 1)])
        with ExitStack() as over:
            xd = over.enter_context(nc.sbuf_tensor("xd", [128, Q], F32))
            zn = over.enter_context(nc.sbuf_tensor("zn", [W, H, C], F32))
            xt = over.enter_context(nc.sbuf_tensor("xt", [H, W, C], F32))
            d1 = over.enter_context(nc.sbuf_tensor("d1", [H, C * W], F32))
            res = over.enter_context(nc.sbuf_tensor("res", [H, C * W], F32))
        wimg = sb("wimg", [96, L + 2 * (WL + 1)])
        wim = sb("wim", [128, L])
        wim8 = sb("wim8", [48, L])
        sq = sb("sq", [128, L])
        sq8 = sb("sq8", [CR, L])
        v = sb("v", [128, 3 * VROW])
        vc = sb("vc", [C, 3 * VROW])
        vp = sb("vp", [128, 2, 128])
        vcp = sb("vcp", [C, 2, 128])
        ww = sb("ww", [96, 3, 6, 128], F32R)

        ps = pb("ps", [128, 2, 512])
        pt = pb("pt", [128, LT, 128])
        pr = pb("pr", [LREM, 512])
        pa = pb("pa", [128, 2, 512])
        pm = pb("pm", [128, 2, 512])

        s_par = sem("params_in")
        s_cos = sem("cos_in")
        s_x = sems("x_in")
        s_mim = sems("match_im2col_in")
        s_wim = sems("ref_im2col_in")
        s_out = sem("stored")
        s_const = sem("constants")
        s_bd6 = sem("output_bias")
        dve_chain = sem("dve_chain")
        pool_chain = sem("pool_chain")
        s_wst = sem("conv_weights_split")
        s_ww = sem("tap_weights_laid")
        s_var = sems("variance")
        s_root = sems("root")
        s_xn = sems("xn_ready")
        s_x3h = sems("x3_high")
        s_x3 = sems("x3_ready")
        s_xres = sems("x_plus_bias")
        s_mf = sem("misc_full")
        s_free = {"act": sem("misc_emptied_act"), "dve": sem("misc_emptied_dve")}
        s_zf = sem("prelu_done")
        s_ef = sem("embed_split")
        s_wimg = sems("ref_image")
        s_mimg = sems("match_image")
        s_epad = sems("embed_padding")
        s_sq = sems("squares")
        s_w = sems("keys_ready")
        s_vf = sems("tap_sums_ready")
        s_kh = sem("tap_high")
        s_split = sem("query_split")
        s_sc = sem("scores")
        s_mx = sem("max")
        s_ex = sem("exp")
        s_pn = sem("softmax")
        s_tr = sem("transposed")
        s_eh = sem("y_high")
        s_el = sem("y_low")
        s_rh = sem("y_last_high")
        s_rl = sem("y_last_low")
        s_pad0 = sem("window_padding")
        s_hn = sem("row_behind_copied")
        s_hp = sem("rows_before_copied")
        s_yc = sem("column_copied")
        s_mn = sem("taps_done")
        s_fin = sem("x1_chunk")
        s_x1 = sems("x1_ready")
        s_var2 = sems("variance2")
        s_root2 = sems("root2")
        s_xd = sems("x1_normalised")

        block = ctx.enter_context(nc.Block())

        def F(ap):
            return ap.bitcast(F32)

        def wait_emptied(eng, name, b, i):
            who, count = emptied(misc_no[name, b, i])
            eng.wait_ge(s_free[who], count)

        def group(eng, name, b, i):
            n = misc_no[name, b, i]
            eng.wait_ge(s_mf, n + 1)
            return pm[:, n % 2, :]

        x3v = x3[:, :].rearrange("p (i s j u) -> p i s j u", s=2, j=WL, u=2)
        e3v = e3[:, :].rearrange("p (i j) -> p i j", j=EW)
        e3f = F(e3[:, :])

        def x1(b):
            return v2[64 + C * b:64 + C * (b + 1), :]

        @block.sync
        def _(sp):
            sp.dma_start(par[:, :], params).then_inc(s_par, 16)

            def load_x(b):
                if b:
                    sp.wait_ge(s_mf, misc_no["u", b - 1, 7] + 1)
                src = x[b].rearrange("c h w -> c (h w)")
                for r in range(3):
                    sp.dma_start(xn[C * r:C * (r + 1), :], src).then_inc(s_x[b], 16)
                sp.dma_start(x1(b), src).then_inc(s_x[b], 16)

            def im2col(b, image, ready, row, size, full, last, done):
                sp.wait_ge(s_const, 6)
                sp.wait_ge(ready, 1)
                for u, (dy, dx) in enumerate(UNITS):
                    at, k = row + 1 + dy * row + dx, 32 * VARIANT[dx]
                    src = image[k:k + CR, at:at + size]
                    for dst in ([full[CR * u:CR * (u + 1), :]] if u < 8 else [last[CR * n:CR * (n + 1), :] for n in range(3)]):
                        sp.dma_start(dst, src).then_inc(done, 16)

            for b in range(B):
                load_x(b)
                if not b:
                    sp.dma_start(cosm[:, :], dct).then_inc(s_cos, 16)
                if b:
                    sp.wait_ge(s_w[b - 1], 1)
                im2col(b, wimg, s_wimg[b], WL, L, wim, wim8, s_wim[b])
                if b:
                    sp.wait_ge(s_split, NCH * b)
                im2col(b, mimg, s_mimg[b], W, Q, vim, v2, s_mim[b])
            for b in range(B):
                for i in range(4):
                    wait_emptied(sp, "d2", b, i)
                    sp.dma_start(out[b, 8 * i:8 * i + 8].rearrange("c k l -> k c l"),
                                 res[:, CHUNK * i:CHUNK * (i + 1)].rearrange("k (c l) -> k c l", l=W)).then_inc(s_out, 16)
            sp.wait_ge(s_out, 16 * 4 * B)

        @block.gpsimd
        def _(pool):
            chain = [0]

            def link(ins):
                chain[0] += 1
                ins.then_inc(pool_chain, 1)
                pool.wait_ge(pool_chain, chain[0])

            link(pool.memset(ident[:, :], 0.0))
            pool.affine_select(out=ident[:, :], in_=ident[:, :], compare_op=ALU.not_equal, fill=1.0, base=0,
                               pattern=[[-1, 128]], channel_multiplier=1).then_inc(s_const, 1)
            pool.memset(ones[:, :], 1.0).then_inc(s_const, 1)
            link(pool.memset(F(ycol[:, :, :, :, :]), 0.0))
            pool.memset(mimg[:, 0:W + 1], 0.0).then_inc(s_const, 1)
            pool.memset(mimg[:, W + 1 + Q:], 0.0).then_inc(s_const, 1)
            pool.memset(wimg[:, 0:WL + 1], 0.0).then_inc(s_const, 1)
            pool.memset(wimg[:, WL + 1 + L:], 0.0).then_inc(s_const, 1)

            def embed_padding(b):
                pool.wait_ge(s_x3[b], 1)
                pool.wait_ge(s_x3h[b], 1)
                pool.memset(e3f[:, 0:2 * EW + 2], 0.0).then_inc(s_epad[b], 1)
                pool.memset(e3f[:, (EW - 2) * EW - 2:], 0.0).then_inc(s_epad[b], 1)
                sides = e3f[:, 2 * EW + 50:2 * EW + 50 + EW * (H - 1)].rearrange("p (i j) -> p i j", j=EW)[:, :, 0:4]
                pool.memset(sides, 0.0).then_inc(s_epad[b], 1)

            def embed_split(b):
                for i in range(NCH):
                    k = conv_no("conva", b, i)
                    dst = e3v[:, 2 + ROWS * i:2 + ROWS * (i + 1), 2:2 + W]
                    src = z[:, k % 2, :].rearrange("p (i j) -> p i j", j=W)
                    pool.wait_ge(s_zf, k + 1)
                    link(pool.tensor_copy(dst, src))
                    pool.tensor_tensor(dst[64:96], src[64:96], F(e3v[64:96, 2 + ROWS * i:2 + ROWS * (i + 1), 2:2 + W]),
                                       ALU.subtract).then_inc(s_ef, 1)
                    pool.wait_ge(s_ef, NCH * b + i + 1)

            def query_split(g):
                b, i, k = g // NCH, g % NCH, g % 2
                cols = slice(CHUNK * i, CHUNK * (i + 1))
                if i == 0:
                    pool.wait_ge(s_mim[b], 16 * 11)
                if g >= 2:
                    pool.wait_ge(s_sc, TPC * (g - 1))
                link(pool.tensor_copy(mh[:, k, :], vim[:, cols]))
                link(pool.tensor_tensor(ml[:, k, :], vim[:, cols], F(mh[:, k, :]), ALU.subtract))
                link(pool.tensor_copy(mr[:, k, :], v2[0:48, cols]))
                pool.tensor_tensor(mr[32:48, k, :], v2[32:48, cols], F(mr[32:48, k, :]), ALU.subtract).then_inc(s_split, 1)
                pool.wait_ge(s_split, g + 1)

            def first_padding(g):
                k = g % 2
                if g >= 2:
                    pool.wait_ge(s_mn, g - 1)
                counted(pool.memset(F(y[:, k, :, 0:LT, 0:PADC]), 0.0), "pad0", s_pad0)
                counted(pool.memset(F(y[0:LREM, k, :, LT, 0:PADC]), 0.0), "pad0", s_pad0)
                counted(pool.memset(F(y[LREM:128, k, :, LT, 0:W]), 0.0), "pad0", s_pad0)

            def last_padding(g):
                counted(pool.memset(F(y[:, g % 2, :, 0:LT, PADC + CHUNK:]), 0.0), "hn", s_hn)
                counted(pool.memset(F(y[LREM:128, g % 2, :, LT, W + CHUNK:WIN - W]), 0.0), "hn", s_hn)

            def row_behind(g):
                k, n = g % 2, (g + 1) % 2
                counted(pool.tensor_copy(y[:, k, :, 0:LT, PADC + CHUNK:], F(y[:, n, :, 0:LT, PADC:PADC + W])), "hn", s_hn)

            def row_behind_last(g):
                k, n = g % 2, (g + 1) % 2
                counted(pool.tensor_copy(y[LREM:128, k, :, LT, W + CHUNK:WIN - W], F(y[LREM:128, n, :, LT, W:2 * W])), "hn", s_hn)

            def rows_before(g):
                k, n = g % 2, (g - 1) % 2
                if g >= 2:
                    pool.wait_ge(s_mn, g - 1)
                counted(pool.tensor_copy(y[:, k, :, 0:LT, 0:PADC], F(y[:, n, :, 0:LT, CHUNK:CHUNK + PADC])), "hp", s_hp)
                counted(pool.tensor_copy(y[0:LREM, k, :, LT, 0:PADC], F(y[0:LREM, n, :, LT, CHUNK:CHUNK + PADC])), "hp", s_hp)
                counted(pool.tensor_copy(y[LREM:128, k, :, LT, 0:W], F(y[LREM:128, n, :, LT, CHUNK:CHUNK + W])), "hp", s_hp)

            def column(g):
                b, i, k = g // NCH, g % NCH, g % 2
                for rows, blocks, at, to in ((slice(0, 128), slice(0, LT), PADC, 2), (slice(0, LREM), slice(LT, LT + 1), PADC, 2),
                                             (slice(LREM, 128), slice(LT, LT + 1), W, 1)):
                    for hl in range(2):
                        src = F(y[rows, k, hl, blocks, at:at + CHUNK:W])
                        dst = ycol[rows, b, hl, blocks, to + ROWS * i:to + ROWS * (i + 1)]
                        counted(pool.tensor_copy(dst, src), "yc", s_yc)
                if i == 0:
                    for hl in range(2):
                        counted(pool.tensor_copy(ycol[:, b, hl, 0:LT, H + 4:H + 5], F(y[:, k, hl, 0:LT, PADC:PADC + 1])), "yc", s_yc)
                        counted(pool.tensor_copy(ycol[0:LREM, b, hl, LT, H + 4:H + 5], F(y[0:LREM, k, hl, LT, PADC:PADC + 1])), "yc", s_yc)

            counts = dict(hn=0, hp=0, yc=0, pad0=0)

            def counted(ins, name, sm):
                counts[name] += 1
                ins.then_inc(sm, 1)
                pool.wait_ge(sm, counts[name])

            embed_padding(0)
            embed_split(0)
            first_padding(0)
            query_split(0)
            query_split(1)
            for s in range(NT):
                g, j = s // TPC, s % TPC
                i = g % NCH
                if s == CONV_STEP:
                    embed_padding(1)
                if s == CONVA_STEP:
                    embed_split(1)
                if j == 0:
                    pool.wait_ge(s_el, s + 1)
                    if i:
                        row_behind(g - 1)
                    elif g:
                        first_padding(g)
                        last_padding(g - 1)
                if j == 0 and i:
                    rows_before(g)
                if j == 2:
                    pool.wait_ge(s_el, s + 1)
                    pool.wait_ge(s_rl, 2 * (g + 1))
                    if i:
                        row_behind_last(g - 1)
                    column(g)
                if (s + 4) % TPC == 0 and 2 <= (s + 4) // TPC < NG:
                    query_split((s + 4) // TPC)
            pool.wait_ge(s_rl, 2 * NG)
            last_padding(NG - 1)

        @block.tensor
        def _(pe):
            def misc(name, b, i):
                n = misc_no[name, b, i]
                if n >= 2:
                    wait_emptied(pe, *plan[n - 2][:3])
                return pm[:, n % 2, :]

            def conv2(b):
                pe.wait_ge(s_wst, 1)
                pe.wait_ge(s_x3[b], 1)
                for i in range(2):
                    o = misc("conv2", b, i)
                    for n in range(4):
                        last = nc.tensor.matmul(o[0:96, 0:HALF], wst[:, P_W2:P_W2 + 96],
                                                x3v[:, HL // 2 * i:HL // 2 * (i + 1), n // 2, :, n % 2],
                                                start=n == 0, stop=n == 3)
                    last.then_inc(s_mf, 1)

            def conv(name, at, b):
                for i in range(NCH):
                    o = misc(name, b, i)
                    nc.tensor.matmul(o[0:96, 0:CHUNK], wst[:, at:at + 96], x3[:, CHUNK * i:CHUNK * (i + 1)],
                                     start=True, stop=True).then_inc(s_mf, 1)

            def norm(b):
                pe.wait_ge(s_sq[b], 2)
                pe.wait_ge(s_const, 2)
                for i in range(2):
                    o = misc("norm", b, i)
                    cols = slice(HALF * i, HALF * (i + 1))
                    nc.tensor.matmul(o[:, 0:HALF], ones[:, :], sq[:, cols], start=True, stop=False)
                    nc.tensor.matmul(o[:, 0:HALF], ones[0:CR, :], sq8[:, cols], start=False, stop=True).then_inc(s_mf, 1)

            def tap_sums(b):
                pe.wait_ge(s_ef, NCH * (b + 1))
                pe.wait_ge(s_epad[b], 3)
                pe.wait_ge(s_ww, 4)
                for n in range(8):
                    column, beta, half = n // 4, n // 2 % 2, n % 2
                    o = misc("u", b, n)
                    m = C if column else 128
                    terms = [(a, kx) for a in ((1, 2) if beta else (0,)) for kx in ((1,) if column else range(6))]
                    for k, (a, kx) in enumerate(terms):
                        r = MY * half + (1, 0, 1)[a]
                        lhs = ww[:, a, 5, 0:C] if column else ww[:, a, kx, :]
                        last = nc.tensor.matmul(o[0:m, 0:VHALF], lhs, e3v[:, r:r + MY - 1:2, kx:kx + W - 1:2],
                                                start=k == 0, stop=k == len(terms) - 1)
                    last.then_inc(s_mf, 1)

            def tap_blocks(b, name, groups, src, pair, size):
                for n, group in enumerate(groups):
                    o = misc(name, b, n)
                    for k, idx in enumerate(group):
                        if idx < PAIR:
                            kind, off = TAP_SRC[idx // LT]
                            at = VROW * kind + off + 128 * (idx % LT)
                            blk = src[:, at:at + 128]
                        elif idx < TOP:
                            blk = pair[:, idx - PAIR, :]
                        else:
                            blk = src[:, 128 * (idx - TOP):128 * (idx - TOP) + 128]
                        last = nc.tensor.transpose(o[:, size * k:size * (k + 1)], blk, ident[0:size, 0:size])
                    last.then_inc(s_mf, 1)

            def taps(b):
                pe.wait_ge(s_vf[b], 8)
                tap_blocks(b, "k", K_GROUPS, v, vp, 128)
                tap_blocks(b, "kc", KC_GROUPS, vc, vcp, C)

            def scores(t):
                g = t // TPC
                b, k = t // (NT // B), g % 2
                cols = slice(128 * (t % TPC), 128 * (t % TPC + 1))
                pe.wait_ge(s_split, g + 1)
                if t % (NT // B) == 0:
                    pe.wait_ge(s_w[b], 1)
                if t:
                    pe.wait_ge(s_ex, t)
                pairs = ((mh, wh), (mh, wl), (ml, wh), (mr, wr))
                for n, (m, w) in enumerate(pairs):
                    for i in range(2):
                        last = nc.tensor.matmul(ps[:, i, 0:HALF], m[:, k, cols], w[b][:, HALF * i:HALF * (i + 1)],
                                                start=n == 0, stop=n == 3)
                last.then_inc(s_sc, 1)

            def transpose(t):
                k, j = t % 2, t % TPC
                pe.wait_ge(s_pn, t + 1)
                if t:
                    pe.wait_ge(s_el, t)
                if j == 0 and t:
                    pe.wait_ge(s_rl, 2 * (t // TPC))
                for i in range(LT):
                    nc.tensor.transpose(pt[:, i, :], p[:, k, 128 * i:128 * (i + 1)], ident[:, :])
                nc.tensor.transpose(pr[:, 128 * j:128 * (j + 1)], p[:, k, 128 * LT:L], ident[:, :]).then_inc(s_tr, 1)

            def tap_list(g):
                b, k = g // NCH, g % 2
                found = []
                def add(idx, blk, off, width, rows=128):
                    kk = [t[b][0:rows, idx, :] for t in (kh, kl)]
                    yy = [y[0:rows, k, hl, blk, off:off + width] for hl in range(2)]
                    found.append((kk[0], yy[0], width))
                    found.append((kk[0], yy[1], width))
                    found.append((kk[1], yy[0], width))
                for di in range(NDJ):
                    if di == 2:
                        add(PAIR, LT, 0, CHUNK)
                        if g % NCH == 0:
                            for i in range(LT + 1):
                                add(TOP + i, i, PADC, W, 128 if i < LT else LREM)
                    for i in range(LT):
                        add(LT * di + i, i, W * di, CHUNK)
                add(PAIR + 1, LT, PADC, CHUNK)
                return found

            def main(g, part):
                b, i = g // NCH, g % NCH
                if part == 0:
                    if i == 0:
                        wait_emptied(pe, "kc", b, 2)
                        pe.wait_ge(s_pad0, 3 * (b + 1))
                    else:
                        pe.wait_ge(s_hp, 3 * (g - b))
                    pe.wait_ge(s_rl, 2 * (g + 1))
                    if g >= 2:
                        pe.wait_ge(s_fin, 4 * (g - 1))
                work = tap_list(g)
                size = len(work) // 3
                if part == 2:
                    pe.wait_ge(s_hn, 2 * (g + 1))
                for n in range(size * part, size * (part + 1)):
                    lhs, rhs, width = work[n]
                    last = nc.tensor.matmul(pa[:, g % 2, 0:width], lhs, rhs, start=n == 0, stop=n == len(work) - 1)
                if part == 2:
                    last.then_inc(s_mn, 1)

            def column_off(b):
                pe.wait_ge(s_yc, column_copies(NCH * (b + 1) - 1))
                o = misc("cc", b, 0)
                work = []
                for idx in range(NK):
                    if idx < PAIR:
                        rows, blk, at, width = 128, idx % LT, idx // LT, H
                    elif idx < TOP:
                        rows, blk, at, width = 128, LT, 2 * (idx - PAIR), H
                    else:
                        rows, blk, at, width = (128 if idx - TOP < LT else LREM), idx - TOP, H + 4, 2
                    for kk, hl in ((kch, 0), (kch, 1), (kcl, 0)):
                        work.append((kk[b][0:rows, idx, :], ycol[0:rows, b, hl, blk, at:at + width], width))
                for n, (lhs, rhs, width) in enumerate(work):
                    last = nc.tensor.matmul(o[0:C, 0:width], lhs, rhs, start=n == 0, stop=n == len(work) - 1)
                last.then_inc(s_mf, 1)

            def cosines(b):
                part = slice(64 + C * b, 64 + C * (b + 1))
                one = ident[part, part]
                pe.wait_ge(s_xd[b], 1)
                for name, src in (("zn", xd[part, :].rearrange("c (h w) -> c h w", w=W)),
                                  ("xt", v2[part, :].rearrange("c (h w) -> c w h", w=W))):
                    for i in range(3):
                        o = misc(name, b, i)
                        for k in range(16):
                            last = nc.tensor.transpose(o[0:W, C * k:C * (k + 1)], src[:, 16 * i + k, :], one)
                        last.then_inc(s_mf, 1)
                pe.wait_ge(s_cos, 16)
                wait_emptied(pe, "zn", b, 2)
                for i in range(4):
                    o = misc("d1", b, i)
                    for k in range(8):
                        last = nc.tensor.matmul(o[0:H, W * k:W * (k + 1)], zn[:, :, 8 * i + k], cosm[:, :], start=True, stop=True)
                    last.then_inc(s_mf, 1)
                for i in range(4):
                    wait_emptied(pe, "d1", b, i)
                    o = misc("d2", b, i)
                    nc.tensor.matmul(o[0:H, 0:CHUNK], cosm[:, :], d1[:, CHUNK * i:CHUNK * (i + 1)],
                                     start=True, stop=True).then_inc(s_mf, 1)

            conv2(0)
            conv("conv1", P_W1, 0)
            conv("conva", P_WA, 0)
            norm(0)
            scores(0)
            for s in range(NT + LAG):
                if s + 1 < NT:
                    scores(s + 1)
                g = (s - LAG) // TPC
                if s >= LAG and g < NG:
                    main(g, (s - LAG) % TPC)
                if s == 0:
                    tap_sums(0)
                if s == 1:
                    taps(0)
                if s == CONV_STEP:
                    conv2(1)
                    conv("conv1", P_W1, 1)
                if s == CONVA_STEP:
                    conv("conva", P_WA, 1)
                if s == NORM_STEP:
                    norm(1)
                if s == SUMS_STEP:
                    tap_sums(1)
                if s == TAPS_STEP:
                    taps(1)
                if s == COL_STEP:
                    column_off(0)
                if s == COS_STEP:
                    cosines(0)
                if s < NT:
                    transpose(s)
            column_off(1)
            cosines(1)

        @block.scalar
        def _(act):
            def root(b):
                act.wait_ge(s_var[b], 1)
                nc.scalar.activation(mv[:, 2:3], mv[:, 1:2], ACT.Sqrt).then_inc(s_root[b], 1)

            def x3_high(b):
                act.wait_ge(s_xn[b], 1)
                if b:
                    act.wait_ge(s_mf, misc_no["conva", b - 1, NCH - 1] + 1)
                nc.scalar.activation(x3[:, :], xn[:, :], ACT.Copy).then_inc(s_x3h[b], 1)

            def residual(b):
                act.wait_ge(s_x[b], 16 * 4)
                act.wait_ge(s_bd6, 1)
                part = slice(64 + C * b, 64 + C * (b + 1))
                nc.scalar.activation(v2[part, :], v2[part, :], ACT.Identity, bias=bd6[part, 0:1]).then_inc(s_xres[b], 1)

            def conv_sums(name, b, n, width, bias, scale=1.0):
                for i in range(n):
                    o = group(act, name, b, i)
                    k = conv_no(name, b, i)
                    if k >= 2:
                        act.wait_ge(s_zf, k - 1)
                        if embed_splits(k - 2):
                            act.wait_ge(s_ef, embed_splits(k - 2))
                    nc.scalar.activation(z[:, k % 2, 0:width], o[0:96, 0:width], ACT.Identity,
                                         bias=par[0:96, bias:bias + 1], scale=scale).then_inc(s_free["act"], 1)

            def squares(b):
                act.wait_ge(s_wim[b], 16 * 11)
                nc.scalar.activation(sq[:, :], wim[:, :], ACT.Square).then_inc(s_sq[b], 1)
                nc.scalar.activation(sq8[:, :], wim8[0:CR, :], ACT.Square).then_inc(s_sq[b], 1)

            def norms(b):
                for i in range(2):
                    o = group(act, "norm", b, i)
                    nc.scalar.activation(sq[:, HALF * i:HALF * (i + 1)], o[:, 0:HALF], ACT.Sqrt).then_inc(s_free["act"], 1)

            def tap_sums(b):
                if b:
                    act.wait_ge(s_mf, misc_no["kc", b - 1, 2] + 1)
                for n in range(8):
                    o = group(act, "u", b, n)
                    dst = vc if n // 4 else v
                    at = VROW * (BETA if n // 2 % 2 else ALPHA) + VHALF * (n % 2)
                    rows = C if n // 4 else 128
                    nc.scalar.activation(dst[:, at:at + VHALF], o[0:rows, 0:VHALF], ACT.Copy).then_inc(s_free["act"], 1)

            def taps_high(b):
                if b:
                    act.wait_ge(s_mim[b], 16 * 11)
                for name, groups, dst, size in (("k", K_GROUPS, kh[b], 128), ("kc", KC_GROUPS, kch[b], C)):
                    for n, blocks in enumerate(groups):
                        o = group(act, name, b, n)
                        sign = -1.0 if blocks[0] >= TOP else 1.0
                        nc.scalar.activation(dst[:, blocks[0]:blocks[-1] + 1, :], grouped(o, blocks, size), ACT.Copy,
                                             scale=sign).then_inc(s_kh, 1)

            def exp(t):
                act.wait_ge(s_mx, t + 1)
                if t >= 2:
                    act.wait_ge(s_tr, t - 1)
                nc.scalar.activation(p[:, t % 2, :].rearrange("p (a c) -> p a c", a=2), ps[:, :, 0:HALF], ACT.Exp,
                                     bias=negm[:, t % 2:t % 2 + 1], accum_out=psm[:, t % 2:t % 2 + 1]).then_inc(s_ex, 1)

            def y_high(t):
                g, j, k = t // TPC, t % TPC, t // TPC % 2
                act.wait_ge(s_tr, t + 1)
                if j == 0 and g >= 2:
                    act.wait_ge(s_mn, g - 1)
                    act.wait_ge(s_hp, 3 * (g - 1 - (g - 1) // NCH))
                    act.wait_ge(s_yc, column_copies(g - 2))
                at = PADC + 128 * j
                nc.scalar.activation(y[:, k, 0, 0:LT, at:at + 128], pt[:, :, :], ACT.Copy).then_inc(s_eh, 1)
                if j == TPC - 1:
                    nc.scalar.activation(y[0:LREM, k, 0, LT, PADC:PADC + CHUNK], pr[:, 0:CHUNK], ACT.Copy).then_inc(s_rh, 1)
                    nc.scalar.activation(y[LREM:128, k, 0, LT, W:W + CHUNK], pr[:, 0:CHUNK], ACT.Copy).then_inc(s_rh, 1)

            def cosines(b):
                for i in range(3):
                    o = group(act, "zn", b, i)
                    nc.scalar.activation(zn[:, 16 * i:16 * (i + 1), :], o[0:W, 0:512].rearrange("w (h c) -> w h c", c=C),
                                         ACT.Copy).then_inc(s_free["act"], 1)
                for i in range(4):
                    o = group(act, "d1", b, i)
                    nc.scalar.activation(d1[:, CHUNK * i:CHUNK * (i + 1)], o[0:H, 0:CHUNK], ACT.Copy).then_inc(s_free["act"], 1)

            def root2(b):
                act.wait_ge(s_var2[b], 1)
                part = slice(64 + C * b, 64 + C * (b + 1))
                nc.scalar.activation(mv2[part, 2:3], mv2[part, 1:2], ACT.Sqrt).then_inc(s_root2[b], 1)

            root(0)
            x3_high(0)
            conv_sums("conv2", 0, 2, HALF, P_B2, 0.25)
            conv_sums("conv1", 0, NCH, CHUNK, P_B1)
            conv_sums("conva", 0, NCH, CHUNK, P_BA)
            residual(0)
            squares(0)
            norms(0)
            exp(0)
            for s in range(NT):
                if s + 1 < NT:
                    exp(s + 1)
                if s == 0:
                    tap_sums(0)
                if s == 1:
                    taps_high(0)
                if s == PREP_STEP:
                    root(1)
                    x3_high(1)
                    residual(1)
                if s == CONV_STEP:
                    conv_sums("conv2", 1, 2, HALF, P_B2, 0.25)
                    conv_sums("conv1", 1, NCH, CHUNK, P_B1)
                if s == CONVA_STEP:
                    conv_sums("conva", 1, NCH, CHUNK, P_BA)
                if s == NORM_STEP:
                    squares(1)
                    norms(1)
                if s == SUMS_STEP:
                    tap_sums(1)
                if s == TAPS_STEP:
                    taps_high(1)
                if s == COL_STEP:
                    root2(0)
                if s == COS_STEP:
                    cosines(0)
                y_high(s)
            root2(1)
            cosines(1)

        @block.vector
        def _(dve):
            chain = [0]

            def link(ins):
                chain[0] += 1
                ins.then_inc(dve_chain, 1)
                dve.wait_ge(dve_chain, chain[0])

            def statistics(src, rows, stats, m, var_ready, root_ready):
                for i in range(NCH):
                    link(nc.vector.bn_stats(stats[rows, i, :], src[:, CHUNK * i:CHUNK * (i + 1)]))
                link(nc.vector.bn_aggr(m[rows, 0:2], stats[rows, :, :]))
                nc.vector.tensor_scalar_add(m[rows, 1:2], m[rows, 1:2], GN_EPS).then_inc(var_ready, 1)
                dve.wait_ge(root_ready, 1)
                link(nc.vector.reciprocal(m[rows, 3:4], m[rows, 2:3]))

            def normalise(b):
                dve.wait_ge(s_x[b], 16 * 4)
                statistics(xn, slice(0, 96), bnst, mv, s_var[b], s_root[b])
                nc.vector.tensor_scalar(xn[:, :], xn[:, :], mv[:, 0:1], mv[:, 3:4], ALU.subtract, ALU.mult).then_inc(s_xn[b], 1)
                dve.wait_ge(s_x3h[b], 1)
                nc.vector.tensor_tensor(x3[64:96, :], xn[64:96, :], F(x3[64:96, :]), ALU.subtract).then_inc(s_x3[b], 1)

            def conv_weights():
                dve.wait_ge(s_par, 16)
                nc.vector.tensor_scalar_mul(bd6[64:128, :], par[64:128, P_BD:P_BD + 1], 1.0 / 6.0).then_inc(s_bd6, 1)
                link(nc.vector.tensor_copy(wst[:, :], par[0:96, 0:P_WD]))
                nc.vector.tensor_tensor(wst[32:64, :], par[32:64, 0:P_WD], F(wst[32:64, :]), ALU.subtract).then_inc(s_wst, 1)

            def tap_weights():
                link(nc.vector.memset(F(ww[:, :, :, :]), 0.0))
                wd = par[0:96, P_WD:P_B1].rearrange("c (a b o) -> c a b o", a=3, b=3)
                places = ((0, 5, 0, 1), (1, 3, 0, 3), (2, 1, 0, 3), (3, 0, 1, 2))
                for dj, kx, b0, n in places:
                    link(nc.vector.tensor_copy(ww[:, :, kx:kx + n, C * dj:C * (dj + 1)], wd[:, :, b0:b0 + n, :]))
                for dj, kx, b0, n in places:
                    dst = ww[32:64, :, kx:kx + n, C * dj:C * (dj + 1)]
                    nc.vector.tensor_tensor(dst, wd[32:64, :, b0:b0 + n, :], F(dst), ALU.subtract).then_inc(s_ww, 1)

            def prelu(name, b, i, alpha, dst, width):
                k = conv_no(name, b, i)
                wait_emptied(dve, name, b, i)
                zk = z[:, k % 2, 0:width]
                link(nc.vector.tensor_scalar(zneg[:, 0:width], zk, 0.0, par[0:96, alpha:alpha + 1], ALU.min, ALU.mult))
                nc.vector.scalar_tensor_tensor(out=dst if dst is not None else zk, in0=zk, scalar=0.0, in1=zneg[:, 0:width],
                                               op0=ALU.max, op1=ALU.add).then_inc(s_zf, 1)
                dve.wait_ge(s_zf, k + 1)

            def edges(image, row, size, ready):
                link(nc.vector.memset(image[32:64, 2 * row:2 * row + size:row], 0.0))
                nc.vector.memset(image[64:96, row + 1:row + 1 + size:row], 0.0).then_inc(ready, 1)

            def ref_image(b):
                if b:
                    dve.wait_ge(s_wim[b - 1], 16 * 11)
                for i in range(2):
                    prelu("conv2", b, i, P_A2, wimg[:, WL + 1 + HALF * i:WL + 1 + HALF * (i + 1)], HALF)
                edges(wimg, WL, L, s_wimg[b])

            def match_image(b):
                if b:
                    dve.wait_ge(s_mim[b - 1], 16 * 11)
                for i in range(NCH):
                    prelu("conv1", b, i, P_A1, mimg[:, W + 1 + CHUNK * i:W + 1 + CHUNK * (i + 1)], CHUNK)
                edges(mimg, W, Q, s_mimg[b])

            def embed(b):
                for i in range(NCH):
                    prelu("conva", b, i, P_AA, None, CHUNK)

            def keys(b):
                wait_emptied(dve, "norm", b, 1)
                link(nc.vector.tensor_scalar_max(sq[:, :], sq[:, :], NORM_EPS))
                link(nc.vector.reciprocal(sq[:, :], sq[:, :]))
                link(nc.vector.scalar_tensor_tensor(out=wim[:, :], in0=wim[:, :], scalar=SOFTMAX_SCALE, in1=sq[:, :],
                                                    op0=ALU.mult, op1=ALU.mult))
                link(nc.vector.scalar_tensor_tensor(out=wim8[:, :], in0=wim8[:, :], scalar=SOFTMAX_SCALE, in1=sq[0:48, :],
                                                    op0=ALU.mult, op1=ALU.mult))
                link(nc.vector.tensor_copy(wh[b][:, :], wim[:, :]))
                link(nc.vector.tensor_copy(wr[b][:, :], wim8[:, :]))
                link(nc.vector.tensor_tensor(wl[b][:, :], wim[:, :], F(wh[b][:, :]), ALU.subtract))
                link(nc.vector.tensor_tensor(wr[b][0:32, :], wim8[0:32, :], F(wr[b][0:32, :]), ALU.subtract))
                nc.vector.tensor_copy(wr[b][0:CR, :], wim8[0:CR, :]).then_inc(s_w[b], 1)

            def tap_sums(b):
                wait_emptied(dve, "u", b, 7)
                for src, pair in ((v, vp), (vc, vcp)):
                    full = src[:, VROW * FULL:VROW * FULL + VROW - WL]
                    link(nc.vector.tensor_tensor(full, src[:, 0:VROW - WL], src[:, VROW * BETA + WL:VROW * (BETA + 1)], ALU.add))
                    for di in range(NDJ):
                        kind, off = TAP_SRC[di]
                        at = VROW * kind + off + 128 * LT
                        nc.vector.tensor_copy(pair[:, di // 2, LREM * (di % 2):LREM * (di % 2 + 1)],
                                              src[:, at:at + LREM]).then_inc(s_vf[b], 1)

            def taps_low(b):
                done = 10 * b
                for name, groups, high, low, size in (("k", K_GROUPS, kh[b], kl[b], 128), ("kc", KC_GROUPS, kch[b], kcl[b], C)):
                    for n, blocks in enumerate(groups):
                        o = group(dve, name, b, n)
                        done += 1
                        dve.wait_ge(s_kh, done)
                        cols = slice(blocks[0], blocks[-1] + 1)
                        sign = -1.0 if blocks[0] >= TOP else 1.0
                        nc.vector.scalar_tensor_tensor(out=low[:, cols, :], in0=grouped(o, blocks, size), scalar=sign,
                                                       in1=F(high[:, cols, :]), op0=ALU.mult,
                                                       op1=ALU.subtract).then_inc(s_free["dve"], 1)

            def maximum(t):
                dve.wait_ge(s_sc, t + 1)
                nc.vector.tensor_reduce(negm[:, t % 2:t % 2 + 1], ps[:, :, 0:HALF], AX.XY, ALU.max, negate=True).then_inc(s_mx, 1)

            def softmax(t):
                k = t % 2
                dve.wait_ge(s_ex, t + 1)
                link(nc.vector.reciprocal(rps[:, k:k + 1], psm[:, k:k + 1]))
                nc.vector.tensor_scalar_mul(p[:, k, :], p[:, k, :], rps[:, k:k + 1]).then_inc(s_pn, 1)

            def y_low(t):
                g, j, k = t // TPC, t % TPC, t // TPC % 2
                dve.wait_ge(s_eh, t + 1)
                at = PADC + 128 * j
                nc.vector.tensor_tensor(y[:, k, 1, 0:LT, at:at + 128], pt[:, :, :], F(y[:, k, 0, 0:LT, at:at + 128]),
                                        ALU.subtract).then_inc(s_el, 1)
                if j == TPC - 1:
                    dve.wait_ge(s_rh, 2 * (g + 1))
                    high = F(y[0:LREM, k, 0, LT, PADC:PADC + CHUNK])
                    nc.vector.tensor_tensor(y[0:LREM, k, 1, LT, PADC:PADC + CHUNK], pr[:, 0:CHUNK], high,
                                            ALU.subtract).then_inc(s_rl, 1)
                    nc.vector.tensor_tensor(y[LREM:128, k, 1, LT, W:W + CHUNK], pr[:, 0:CHUNK], high,
                                            ALU.subtract).then_inc(s_rl, 1)

            def finish(g):
                b, i = g // NCH, g % NCH
                dve.wait_ge(s_mn, g + 1)
                if i == 0:
                    dve.wait_ge(s_xres[b], 1)
                rows = x1(b)[:, CHUNK * i:CHUNK * (i + 1)].rearrange("c (i j) -> c i j", j=W)
                for n, dj in enumerate((0, -2, -1, 1)):
                    k = C * (dj + 2)
                    acc = pa[k:k + C, g % 2, 0:CHUNK].rearrange("c (i j) -> c i j", j=W)
                    lo, hi = max(0, -dj), W - max(0, dj)
                    nc.vector.scalar_tensor_tensor(out=rows[:, :, lo:hi], in0=acc[:, :, lo + dj:hi + dj], scalar=1.0 / 6.0,
                                                   in1=rows[:, :, lo:hi], op0=ALU.mult, op1=ALU.add).then_inc(s_fin, 1)
                    dve.wait_ge(s_fin, 4 * g + n + 1)

            def column_off(b):
                o = group(dve, "cc", b, 0)
                col = x1(b)[:, 0:Q:W]
                nc.vector.scalar_tensor_tensor(out=col, in0=o[0:C, 0:H], scalar=-1.0 / 6.0, in1=col, op0=ALU.mult,
                                               op1=ALU.add).then_inc(s_free["dve"], 1)
                wait_emptied(dve, "cc", b, 0)
                rows = slice(64 + C * b, 64 + C * (b + 1))
                statistics(x1(b), rows, bnst2, mv2, s_var2[b], s_root2[b])
                if b:
                    dve.wait_ge(s_mf, misc_no["zn", b - 1, 2] + 1)
                else:
                    dve.wait_ge(s_mf, misc_no["kc", B - 1, 2] + 1)
                    dve.wait_ge(s_wim[B - 1], 16 * 11)
                nc.vector.tensor_scalar(xd[rows, :], x1(b), mv2[rows, 0:1], mv2[rows, 3:4], ALU.subtract,
                                        ALU.mult).then_inc(s_xd[b], 1)

            def cosines(b):
                for i in range(3):
                    o = group(dve, "xt", b, i)
                    nc.vector.tensor_copy(xt[:, 16 * i:16 * (i + 1), :], o[0:H, 0:512].rearrange("h (w c) -> h w c", c=C))\
                        .then_inc(s_free["dve"], 1)
                wait_emptied(dve, "xt", b, 2)
                if b:
                    dve.wait_ge(s_out, 16 * 4 * b)
                for i in range(4):
                    o = group(dve, "d2", b, i)
                    nc.vector.tensor_tensor(res[:, CHUNK * i:CHUNK * (i + 1)].rearrange("k (c l) -> k c l", l=W),
                                            o[0:H, 0:CHUNK].rearrange("k (c l) -> k c l", l=W),
                                            xt[:, :, 8 * i:8 * (i + 1)].rearrange("h w c -> h c w"),
                                            ALU.add).then_inc(s_free["dve"], 1)

            conv_weights()
            normalise(0)
            ref_image(0)
            match_image(0)
            embed(0)
            keys(0)
            tap_weights()
            maximum(0)
            softmax(0)
            for s in range(NT + LAG):
                if s + 1 < NT:
                    maximum(s + 1)
                    softmax(s + 1)
                g = (s - LAG) // TPC
                if s >= LAG and (s - LAG) % TPC == TPC - 1 and g < NG:
                    finish(g)
                if s == 0:
                    tap_sums(0)
                if s == 1:
                    taps_low(0)
                if s == PREP_STEP:
                    normalise(1)
                if s == CONV_STEP:
                    ref_image(1)
                    match_image(1)
                if s == CONVA_STEP:
                    embed(1)
                if s == NORM_STEP:
                    keys(1)
                if s == SUMS_STEP:
                    tap_sums(1)
                if s == TAPS_STEP:
                    taps_low(1)
                if s == COL_STEP:
                    column_off(0)
                if s == COS_STEP:
                    cosines(0)
                if s < NT:
                    y_low(s)
            column_off(1)
            cosines(1)


def kernel(**inputs):
    import concourse.bacc as bacc
    from concourse.bass_utils import run_bass_kernel_spmd

    a = {k.replace("L0_conv_", ""): np.asarray(v) for k, v in inputs.items()}
    par = np.zeros((128, NP), np.float32)
    w1t, w2t, wat = a["W1"].T, a["W2"].T, a["Wa"].T
    wdt = a["Wd"].transpose(1, 2, 3, 0).reshape(C, 9 * C)
    for r in range(3):
        rows = slice(32 * r, 32 * (r + 1))
        for k in range(3):
            par[rows, P_W1 + 32 * k:P_W1 + 32 * k + CR] = w1t
            par[rows, P_W2 + 32 * k:P_W2 + 32 * k + CR] = w2t
            par[rows, P_WA + 32 * k:P_WA + 32 * (k + 1)] = wat
        par[rows, P_WD:P_B1] = wdt
        par[32 * r:32 * r + CR, P_B1] = a["b1"]
        par[32 * r:32 * r + CR, P_B2] = a["b2"]
        par[rows, P_BA] = a["ba"]
    par[:, P_A1], par[:, P_A2], par[:, P_AA] = a["a1"][0], a["a2"][0], a["aa"][0]
    for b in range(B):
        par[64 + C * b:64 + C * (b + 1), P_BD] = a["bd"]
    k, n = np.arange(W)[:, None], np.arange(W)[None, :]
    dct = np.cos(np.pi * (2.0 * n + 1.0) * k / (2.0 * W)) * np.where(k == 0, np.sqrt(1.0 / W), np.sqrt(2.0 / W))
    arrays = {"x": np.ascontiguousarray(a["x"]), "params": par, "dct": np.ascontiguousarray(dct.astype(np.float32).T)}

    nc = bacc.Bacc("TRN2", target_bir_lowering=False, num_devices=1)
    ins = [nc.dram_tensor(n, v.shape, F32, kind="ExternalInput").ap() for n, v in arrays.items()]
    out = nc.dram_tensor("out", (B, C, H, W), F32, kind="ExternalOutput").ap()
    program(nc, *ins, out)
    return run_bass_kernel_spmd(nc, [arrays], core_ids=[0]).results[0]["out"]
```

```python
from contextlib import ExitStack

import concourse.bass as bass
import concourse.mybir as mybir
import numpy as np

F32 = mybir.dt.float32
F32R = mybir.dt.float32r
ALU = mybir.AluOpType
ACT = mybir.ActivationFunctionType
AX = mybir.AxisListType

B, C, H, W = 2, 32, 48, 48
CR = C // 2
Q = H * W
HL, WL = H // 2, W // 2
L = HL * WL
HALF = L // 2
ROWS = 8
CHUNK = ROWS * W
NCH = Q // CHUNK
TPC = CHUNK // 128
NT = B * Q // 128
NG = B * NCH
LT = L // 128
LREM = L - 128 * LT
PADC = 2 * W
WIN = PADC + CHUNK + W
NDJ = 4
MY = HL + 2
VROW = MY * WL
VHALF = VROW // 2
EW = W + 4
GN_EPS = 1e-5
NORM_EPS = 1e-4
SOFTMAX_SCALE = 10.0
LAG = 4

NK = 4 * LT + 2 + LT + 1
PAIR, TOP = 4 * LT, 4 * LT + 2
ALPHA, FULL, BETA = 0, 1, 2
TAP_SRC = [(ALPHA, 2 * WL), (FULL, WL), (FULL, 0), (BETA, 0)]

P_W1, P_W2, P_WA, P_WD = 0, 96, 192, 288
P_B1, P_B2, P_BA, P_A1, P_A2, P_AA, P_BD = 576, 577, 578, 579, 580, 581, 582
NP = 584

SHIFTS = [(0, 3), (-1, 3), (1, 2)]
IM2COL = len(SHIFTS) + 3


EMPTIES = {"conv2": "act", "conv1": "act", "conva": "act", "norm": "dve", "inorm": "dve", "u": "act", "k": "dve", "kc": "dve", "cc": "dve",
           "zn": "act", "d1": "act", "d2": "dve"}


def stages(b, *names):
    return [(name, b, i) for name, n in names for i in range(n)]


def side_jobs():
    conva = stages(0, ("conva", NCH))
    before = (stages(0, ("rows", 3), ("scale", 2), ("low", 2), ("conv2", 2), ("conv1", NCH), ("squares", 1)) + conva[:2]
              + [("norm", 0, 0)] + conva[2:3] + [("split", 0, 0)] + stages(0, ("inorm", 2)) + conva[3:4] + [("keys", 0, 0)]
              + conva[4:] + [("split", 0, 1)])
    gaps = {}

    def spread(step, each, jobs, gap=0):
        for n in range(0, len(jobs), each):
            gaps.setdefault(divmod(3 * step + gap + n // each, 3), []).extend(jobs[n:n + each])

    spread(0, 2, stages(0, ("u", 8), ("sums", 2), ("k", 7), ("kc", 3)))
    spread(3, 1, [("load", 1, 0)], 1)
    spread(4, 1, stages(1, ("rows", 3), ("scale", 2), ("low", 2), ("conv2", 2), ("conv1", NCH), ("conva", NCH)), 1)
    spread(5, 1, [("residual", 0, 0)], 0)
    spread(11, 1, stages(1, ("squares", 1)), 1)
    spread(11, 1, stages(1, ("norm", 1)), 2)
    spread(12, 1, stages(1, ("inorm", 2)), 1)
    spread(13, 1, stages(1, ("keys", 1), ("u", 8)), 0)
    spread(16, 1, stages(1, ("sums", 2)), 1)
    spread(17, 1, stages(1, ("k", 7), ("kc", 3), ("residual", 1)), 1)
    for g in range(2, NG):
        spread(TPC * g - 3, 1, [("split", g // NCH, g % NCH)], 1)
    spread(21, 1, stages(0, ("cc", 1), ("stats", 1)), 1)
    for n, job in enumerate(stages(0, ("deviation", 1), ("x1n", 3), ("zn", 3), ("d1", 2), ("d2", 2))):
        spread(24 + n, 1, [job], 2)
    spread(39, 1, stages(1, ("cc", 1), ("stats", 1)))
    behind = stages(1, ("deviation", 1), ("x1n", 3), ("zn", 3), ("d1", 2), ("d2", 2))
    return before, gaps, behind


def conv_no(name, b, i):
    return (2 + 2 * NCH) * b + {"conv2": 0, "conv1": 2, "conva": 2 + NCH}[name] + i


def embed_splits(k):
    b, i = k // (2 + 2 * NCH), k % (2 + 2 * NCH) - (2 + NCH)
    return NCH * b + i + 1 if i >= 0 else 0


def column_copies(g):
    return 6 * (g + 1) + 4 * (g // NCH + 1)


def grouped(bank, blocks, size):
    return bank[:, 0:size * len(blocks)].rearrange("p (n c) -> p n c", c=size)


K_GROUPS = [range(4 * n, 4 * n + 4) for n in range(4)] + [range(PAIR, TOP), range(TOP, TOP + 4), range(TOP + 4, NK)]
KC_GROUPS = [range(0, PAIR), range(PAIR, TOP), range(TOP, NK)]


def program(nc, x, params, dct, x1_copy, out):
    before, gaps, behind = side_jobs()
    steps = NT + LAG
    ordered = before + [job for s in range(steps) for n in range(3) for job in gaps.get((s, n), [])] + behind
    plan = [job for job in ordered if job[0] in EMPTIES]
    misc_no = {job: n for n, job in enumerate(plan)}

    def emptied(n):
        eng = EMPTIES[plan[n][0]]
        return eng, sum(EMPTIES[name] == eng for name, _, _ in plan[:n + 1])

    with ExitStack() as ctx:
        def sb(name, shape, dt=F32):
            return ctx.enter_context(nc.sbuf_tensor(name, shape, dt))

        def pb(name, shape):
            return ctx.enter_context(nc.psum_tensor(name, shape, F32))

        def sem(name):
            return ctx.enter_context(nc.semaphore(name))

        def sems(name, n=B):
            return [sem(f"{name}{i}") for i in range(n)]

        ident = sb("ident", [128, 128])
        ones = sb("ones", [128, 128])
        par = sb("par", [128, NP])
        wst = sb("wst", [96, P_WD], F32R)
        cosm = sb("cosm", [2 * W, 2 * W])
        nbias = sb("nbias", [96, 3])
        nslope = sb("nslope", [96, 3])
        mhalf = sb("mhalf", [128, 1])
        bd6 = sb("bd6", [128, 1])
        bnst = sb("bnst", [96, NCH, 6])
        bnst2 = sb("bnst2", [128, NCH, 6])
        mv2 = sb("mv2", [128, 4])
        mv = sb("mv", [96, 4])
        y = sb("y", [128, 2, 2, LT + 1, WIN], F32R)
        ycol = sb("ycol", [128, B, 2, LT + 1, H + 6], F32R)
        kh = [sb("kh0", [128, NK, 128], F32R)]
        kl = [sb("kl0", [128, NK, 128], F32R)]
        kch = [sb(f"kch{b}", [128, NK, C], F32R) for b in range(B)]
        kcl = [sb(f"kcl{b}", [128, NK, C], F32R) for b in range(B)]
        vim = sb("vim", [128, Q])
        v2 = sb("v2", [128, Q])
        p = sb("p", [128, 2, L])
        mh = sb("mh", [128, 2, CHUNK], F32R)
        ml = sb("ml", [128, 2, CHUNK], F32R)
        mr = sb("mr", [48, 2, CHUNK], F32R)
        wh = [sb(f"wh{b}", [128, L], F32R) for b in range(B)]
        wl = [sb(f"wl{b}", [128, L], F32R) for b in range(B)]
        wr = [sb(f"wr{b}", [48, L], F32R) for b in range(B)]
        negm = sb("negm", [128, 2])
        psm = sb("psm", [128, 2])
        rps = sb("rps", [128, 2])
        z = sb("z", [96, 2, CHUNK])
        zneg = sb("zneg", [96, 2, CHUNK])
        with ExitStack() as over:
            kh.append(over.enter_context(nc.sbuf_tensor("kh1", [128, NK, 128], F32R)))
            kl.append(over.enter_context(nc.sbuf_tensor("kl1", [128, NK, 128], F32R)))
        with ExitStack() as over:
            xn = over.enter_context(nc.sbuf_tensor("xn", [96, Q], F32))
        e3 = sb("e3", [96, EW * EW], F32R)
        x3 = sb("x3", [96, Q], F32R)
        mimg = sb("mimg", [96, Q + 2 * (W + 1)])
        with ExitStack() as over:
            xd = over.enter_context(nc.sbuf_tensor("xd", [128, Q], F32))
            zn = over.enter_context(nc.sbuf_tensor("zn", [W, C, H], F32))
            xr = over.enter_context(nc.sbuf_tensor("xr", [2 * H, C // 2 * W], F32))
            d1 = over.enter_context(nc.sbuf_tensor("d1", [2 * H, C // 2 * W], F32))
            res = over.enter_context(nc.sbuf_tensor("res", [2 * H, C // 2 * W], F32))
        wimg = sb("wimg", [96, L + 2 * (WL + 1)])
        wim = sb("wim", [128, L])
        wim8 = sb("wim8", [48, L])
        sq = sb("sq", [128, L])
        sq8 = sb("sq8", [CR, L])
        nrm = sb("nrm", [96, 12])
        v = sb("v", [128, 3 * VROW])
        vc = sb("vc", [C, 3 * VROW])
        vp = sb("vp", [128, 2, 128])
        vcp = sb("vcp", [C, 2, 128])
        ww = sb("ww", [96, 3, 6, 128], F32R)

        ps = pb("ps", [128, 2, 512])
        pt = pb("pt", [128, LT, 128])
        pr = pb("pr", [LREM, 512])
        pa = pb("pa", [128, 2, 512])
        pm = pb("pm", [128, 2, 512])

        s_par = sem("params_in")
        s_cos = sem("cos_in")
        s_x = sems("x_in")
        s_mim = sems("match_im2col_in")
        s_wim = sems("ref_im2col_in")
        s_out = sem("stored")
        s_const = sem("constants")
        s_bd6 = sem("output_bias")
        dve_chain = sem("dve_chain")
        pool_chain = sem("pool_chain")
        s_wst = sem("conv_weights_split")
        s_ww = sem("tap_weights_laid")
        s_var = sems("variance")
        s_root = sems("inverse_root")
        s_xn = sems("xn_ready")
        s_x3h = sems("x3_high")
        s_x3 = sems("x3_ready")
        s_xres = sems("x_plus_bias")
        s_mf = sem("misc_full")
        s_free = {"act": sem("misc_emptied_act"), "dve": sem("misc_emptied_dve")}
        s_zf = sem("prelu_done")
        s_ef = sem("embed_split")
        s_wimg = sems("ref_image")
        s_mimg = sems("match_image")
        s_epad = sems("embed_padding")
        s_sq = sems("squares")
        s_sqs = sems("squares_joined")
        s_inv = sems("inverse_norms")
        s_whi = sems("keys_high")
        s_w = sems("keys_ready")
        s_vf = sems("tap_sums_ready")
        s_kh = sem("tap_high")
        s_splith = sem("query_high")
        s_split = sem("query_split")
        s_sc = sem("scores")
        s_mx = sem("max")
        s_ex = sem("exp")
        s_pn = sem("softmax")
        s_tr = sem("transposed")
        s_eh = sem("y_high")
        s_el = sem("y_low")
        s_rh = sem("y_last_high")
        s_rl = sem("y_last_low")
        s_pad0 = sem("window_padding")
        s_hn = sem("row_behind_copied")
        s_hp = sem("rows_before_copied")
        s_yc = sem("column_copied")
        s_mn = sem("taps_done")
        s_fin = sem("x1_chunk")
        s_var2 = sems("variance2")
        s_root2 = sems("inverse_root2")
        s_zs = sem("conv_sum_read")
        s_x1out = sems("x1_stored")
        s_xr = sems("residual_in")
        s_nb = sem("negative_constants")
        s_xd = sems("x1_normalised")

        block = ctx.enter_context(nc.Block())

        def F(ap):
            return ap.bitcast(F32)

        def wait_emptied(eng, name, b, i):
            who, count = emptied(misc_no[name, b, i])
            eng.wait_ge(s_free[who], count)

        def group(eng, name, b, i):
            n = misc_no[name, b, i]
            eng.wait_ge(s_mf, n + 1)
            return pm[:, n % 2, :]

        x3v = x3[:, :].rearrange("p (i s j u) -> p i s j u", s=2, j=WL, u=2)
        e3v = e3[:, :].rearrange("p (i j) -> p i j", j=EW)
        e3f = F(e3[:, :])

        def place_free(eng):
            eng.wait_ge(s_mf, misc_no["kc", B - 1, 2] + 1)
            eng.wait_ge(s_wim[B - 1], 16 * IM2COL)

        def perform(jobs, handlers):
            for name, b, i in jobs:
                if name in handlers:
                    handlers[name](b, i)

        def x1(b):
            return v2[64 + C * b:64 + C * (b + 1), :]

        @block.sync
        def _(sp):
            def load_x(b):
                if b:
                    sp.wait_ge(s_mf, misc_no["u", b - 1, 7] + 1)
                src = x[b].rearrange("c h w -> c (h w)")
                for r in range(3):
                    sp.dma_start(xn[C * r:C * (r + 1), :], src).then_inc(s_x[b], 16)
                sp.dma_start(x1(b), src).then_inc(s_x[b], 16)

            def im2col(b, image, ready, row, size, full, last, done):
                sp.wait_ge(s_const, 6)
                sp.wait_ge(ready, 1)
                pitch = image.shape[1]
                for k, (dx, n) in enumerate(SHIFTS):
                    src = image[32 * k:32 * k + CR, 1 + dx:1 + dx + size]
                    src = bass.AP(src.tensor, src.offset, [[pitch, CR], [row, n], [1, size]])
                    dst = full[3 * CR * k:3 * CR * k + n * CR, :]
                    sp.dma_start(dst, src).then_inc(done, 16)
                at = 2 * row + 1 + SHIFTS[2][0]
                src = image[64:64 + CR, at:at + size]
                for n in range(3):
                    sp.dma_start(last[CR * n:CR * (n + 1), :], src).then_inc(done, 16)

            for b in range(B):
                load_x(b)
                if not b:
                    sp.dma_start(par[:, :], params).then_inc(s_par, 16)
                    sp.dma_start(cosm[:, :], dct).then_inc(s_cos, 16)
                if b:
                    sp.wait_ge(s_w[b - 1], 1)
                im2col(b, wimg, s_wimg[b], WL, L, wim, wim8, s_wim[b])
                if b:
                    sp.wait_ge(s_split, NCH * b)
                im2col(b, mimg, s_mimg[b], W, Q, vim, v2, s_mim[b])
            for b in range(B):
                sp.wait_ge(s_fin, 4 * NCH * (b + 1))
                wait_emptied(sp, "cc", b, 0)
                sp.dma_start(x1_copy[b], x1(b)).then_inc(s_x1out[b], 16)
                sp.wait_ge(s_x1out[b], 16)
                if b:
                    wait_emptied(sp, "d2", b - 1, 1)
                else:
                    place_free(sp)
                pairs = x1_copy[b].rearrange("(p t) (h w) -> t h p w", t=2, w=W)
                for t in range(2):
                    sp.dma_start(xr[H * t:H * (t + 1), :].rearrange("h (p w) -> h p w", w=W), pairs[t]).then_inc(s_xr[b], 16)
                for i in range(2):
                    wait_emptied(sp, "d2", b, i)
                    dst = out[b].rearrange("(g p t) k l -> g t k p l", g=2, t=2)
                    for t in range(2):
                        sp.dma_start(dst[i, t], res[H * t:H * (t + 1), CHUNK * i:CHUNK * (i + 1)]
                                     .rearrange("k (p l) -> k p l", l=W)).then_inc(s_out, 16)
            sp.wait_ge(s_out, 16 * 4 * B)

        @block.gpsimd
        def _(pool):
            chain = [0]

            def link(ins):
                chain[0] += 1
                ins.then_inc(pool_chain, 1)
                pool.wait_ge(pool_chain, chain[0])

            link(pool.memset(ident[:, :], 0.0))
            pool.affine_select(out=ident[:, :], in_=ident[:, :], compare_op=ALU.not_equal, fill=1.0, base=0,
                               pattern=[[-1, 128]], channel_multiplier=1).then_inc(s_const, 1)
            pool.memset(ones[:, :], 1.0).then_inc(s_const, 1)
            link(pool.memset(mhalf[:, :], -0.5))
            link(pool.memset(F(ycol[:, :, :, :, :]), 0.0))
            link(pool.memset(F(ww[:, :, :, :]), 0.0))
            pool.memset(mimg[:, 0:W + 1], 0.0).then_inc(s_const, 1)
            pool.memset(mimg[:, W + 1 + Q:], 0.0).then_inc(s_const, 1)
            pool.memset(wimg[:, 0:WL + 1], 0.0).then_inc(s_const, 1)
            pool.memset(wimg[:, WL + 1 + L:], 0.0).then_inc(s_const, 1)

            def inverse_root(m, half, var_ready, ready):
                pool.wait_ge(var_ready, 1)
                pool.tensor_tensor(m[:, 3:4], m[:, 1:2], half, ALU.pow).then_inc(ready, 1)
                pool.wait_ge(ready, 1)

            def tap_weights():
                pool.wait_ge(s_par, 16)
                wd = par[0:96, P_WD:P_B1].rearrange("c (a b o) -> c a b o", a=3, b=3)
                places = ((0, 5, 0, 1), (1, 3, 0, 3), (2, 1, 0, 3), (3, 0, 1, 2))
                for dj, kx, b0, n in places:
                    link(pool.tensor_copy(ww[:, :, kx:kx + n, C * dj:C * (dj + 1)], wd[:, :, b0:b0 + n, :]))
                for dj, kx, b0, n in places:
                    dst = ww[32:64, :, kx:kx + n, C * dj:C * (dj + 1)]
                    pool.tensor_tensor(dst, wd[32:64, :, b0:b0 + n, :], F(dst), ALU.subtract).then_inc(s_ww, 1)
                pool.wait_ge(s_ww, 4)

            def scale(b, i):
                if i == 0:
                    inverse_root(mv[:, :], mhalf[0:96, :], s_var[b], s_root[b])

            def embed_padding(b, i):
                if i == 0:
                    return
                pool.wait_ge(s_x3[b], 2)
                pool.wait_ge(s_x3h[b], 2)
                pool.memset(e3f[:, 0:2 * EW + 2], 0.0).then_inc(s_epad[b], 1)
                pool.memset(e3f[:, (EW - 2) * EW - 2:], 0.0).then_inc(s_epad[b], 1)
                sides = e3f[:, 2 * EW + 50:2 * EW + 50 + EW * (H - 1)].rearrange("p (i j) -> p i j", j=EW)[:, :, 0:4]
                pool.memset(sides, 0.0).then_inc(s_epad[b], 1)
                pool.wait_ge(s_epad[b], 3)

            def embed_low(b, i):
                k = conv_no("conva", b, i)
                rows = e3v[64:96, 2 + ROWS * i:2 + ROWS * (i + 1), 2:2 + W]
                pool.wait_ge(s_zf, k + 1)
                pool.tensor_tensor(rows, z[64:96, k % 2, :].rearrange("p (i j) -> p i j", j=W), F(rows),
                                   ALU.subtract).then_inc(s_ef, 1)
                pool.wait_ge(s_ef, NCH * b + i + 1)

            def inverse_norms(b, _):
                wait_emptied(pool, "norm", b, 0)
                pool.tensor_tensor(nrm[:, 6:12], nrm[:, 0:6], mhalf[0:96, 0:1].to_broadcast([96, 6]), ALU.pow).then_inc(s_inv[b], 1)
                pool.wait_ge(s_inv[b], 1)

            def query_low(b, i):
                g = NCH * b + i
                k = g % 2
                cols = slice(CHUNK * i, CHUNK * (i + 1))
                pool.wait_ge(s_splith, 2 * g + 1)
                link(pool.tensor_tensor(ml[:, k, :], vim[:, cols], F(mh[:, k, :]), ALU.subtract))
                pool.wait_ge(s_splith, 2 * g + 2)
                pool.tensor_tensor(mr[32:48, k, :], v2[32:48, cols], F(mr[32:48, k, :]), ALU.subtract).then_inc(s_split, 1)
                pool.wait_ge(s_split, g + 1)

            def first_padding(g):
                k = g % 2
                if g >= 2:
                    pool.wait_ge(s_mn, g - 1)
                counted(pool.memset(F(y[:, k, :, 0:LT, 0:PADC]), 0.0), "pad0", s_pad0)
                counted(pool.memset(F(y[0:LREM, k, :, LT, 0:PADC]), 0.0), "pad0", s_pad0)
                counted(pool.memset(F(y[LREM:128, k, :, LT, 0:W]), 0.0), "pad0", s_pad0)

            def last_padding(g):
                counted(pool.memset(F(y[:, g % 2, :, 0:LT, PADC + CHUNK:]), 0.0), "hn", s_hn)
                counted(pool.memset(F(y[LREM:128, g % 2, :, LT, W + CHUNK:WIN - W]), 0.0), "hn", s_hn)

            def row_behind(g):
                k, n = g % 2, (g + 1) % 2
                counted(pool.tensor_copy(y[:, k, :, 0:LT, PADC + CHUNK:], F(y[:, n, :, 0:LT, PADC:PADC + W])), "hn", s_hn)

            def row_behind_last(g):
                k, n = g % 2, (g + 1) % 2
                counted(pool.tensor_copy(y[LREM:128, k, :, LT, W + CHUNK:WIN - W], F(y[LREM:128, n, :, LT, W:2 * W])), "hn", s_hn)

            def column(g):
                b, i, k = g // NCH, g % NCH, g % 2
                for rows, blocks, at, to in ((slice(0, 128), slice(0, LT), PADC, 2), (slice(0, LREM), slice(LT, LT + 1), PADC, 2),
                                             (slice(LREM, 128), slice(LT, LT + 1), W, 1)):
                    for hl in range(2):
                        src = F(y[rows, k, hl, blocks, at:at + CHUNK:W])
                        dst = ycol[rows, b, hl, blocks, to + ROWS * i:to + ROWS * (i + 1)]
                        counted(pool.tensor_copy(dst, src), "yc", s_yc)
                if i == 0:
                    for hl in range(2):
                        counted(pool.tensor_copy(ycol[:, b, hl, 0:LT, H + 4:H + 5], F(y[:, k, hl, 0:LT, PADC:PADC + 1])), "yc", s_yc)
                        counted(pool.tensor_copy(ycol[0:LREM, b, hl, LT, H + 4:H + 5], F(y[0:LREM, k, hl, LT, PADC:PADC + 1])), "yc", s_yc)

            counts = dict(hn=0, yc=0, pad0=0)

            def counted(ins, name, sm):
                counts[name] += 1
                ins.then_inc(sm, 1)
                pool.wait_ge(sm, counts[name])

            def deviation(b, i):
                rows = slice(64 + C * b, 64 + C * (b + 1))
                inverse_root(mv2[rows, :], mhalf[rows, :], s_var2[b], s_root2[b])

            handlers = {"scale": scale, "low": embed_padding, "norm": inverse_norms, "conva": embed_low, "split": query_low,
                        "deviation": deviation}
            first = before.index(("scale", 0, 1))
            perform(before[:first], handlers)
            tap_weights()
            perform(before[first:], handlers)
            first_padding(0)
            for s in range(steps):
                for n in range(3):
                    perform(gaps.get((s, n), []), handlers)
                if s >= NT:
                    continue
                g, j = s // TPC, s % TPC
                i = g % NCH
                if j == 0:
                    pool.wait_ge(s_el, s + 1)
                    if i:
                        row_behind(g - 1)
                    elif g:
                        first_padding(g)
                        last_padding(g - 1)
                if j == 2:
                    pool.wait_ge(s_el, s + 1)
                    pool.wait_ge(s_rl, 2 * (g + 1))
                    if i:
                        row_behind_last(g - 1)
                    column(g)
                if s == NT - 1:
                    last_padding(NG - 1)
            perform(behind, handlers)

        @block.tensor
        def _(pe):
            def misc(name, b, i):
                n = misc_no[name, b, i]
                if n >= 2:
                    wait_emptied(pe, *plan[n - 2])
                return pm[:, n % 2, :]

            def conv2(b, i):
                if b == 0:
                    pe.wait_ge(s_wst, 1)
                pe.wait_ge(s_x3[b], i + 1)
                o = misc("conv2", b, i)
                for n in range(4):
                    last = nc.tensor.matmul(o[0:96, 0:HALF], wst[:, P_W2:P_W2 + 96],
                                            x3v[:, HL // 2 * i:HL // 2 * (i + 1), n // 2, :, n % 2],
                                            start=n == 0, stop=n == 3)
                last.then_inc(s_mf, 1)

            def conv(name, at, b, i):
                o = misc(name, b, i)
                nc.tensor.matmul(o[0:96, 0:CHUNK], wst[:, at:at + 96], x3[:, CHUNK * i:CHUNK * (i + 1)],
                                 start=True, stop=True).then_inc(s_mf, 1)

            def norm(b, _):
                pe.wait_ge(s_sqs[b], 1)
                pe.wait_ge(s_const, 2)
                o = misc("norm", b, 0)
                for n in range(6):
                    cols = slice(96 * n, 96 * (n + 1))
                    last = nc.tensor.matmul(o[0:96, n:n + 1], sq[:, cols], ones[:, 0:1], start=True, stop=True)
                last.then_inc(s_mf, 1)

            def inverse_norms(b, i):
                pe.wait_ge(s_inv[b], 1)
                o = misc("inorm", b, i)
                for n in range(3):
                    last = nc.tensor.matmul(o[:, 96 * n:96 * (n + 1)],
                                            nrm[:, 6 + 3 * i + n:7 + 3 * i + n].to_broadcast([96, 128]), ident[0:96, 0:96],
                                            start=True, stop=True)
                last.then_inc(s_mf, 1)

            def tap_sums(b, n):
                pe.wait_ge(s_ef, NCH * (b + 1))
                pe.wait_ge(s_epad[b], 3)
                pe.wait_ge(s_ww, 4)
                column, beta, half = n // 4, n // 2 % 2, n % 2
                o = misc("u", b, n)
                m = C if column else 128
                terms = [(a, kx) for a in ((1, 2) if beta else (0,)) for kx in ((1,) if column else range(6))]
                for k, (a, kx) in enumerate(terms):
                    r = MY * half + (1, 0, 1)[a]
                    lhs = ww[:, a, 5, 0:C] if column else ww[:, a, kx, :]
                    last = nc.tensor.matmul(o[0:m, 0:VHALF], lhs, e3v[:, r:r + MY - 1:2, kx:kx + W - 1:2],
                                            start=k == 0, stop=k == len(terms) - 1)
                last.then_inc(s_mf, 1)

            def tap_blocks(name, b, n):
                pe.wait_ge(s_vf[b], 8)
                groups, src, pair, size = (K_GROUPS, v, vp, 128) if name == "k" else (KC_GROUPS, vc, vcp, C)
                o = misc(name, b, n)
                for k, idx in enumerate(groups[n]):
                    if idx < PAIR:
                        kind, off = TAP_SRC[idx // LT]
                        at = VROW * kind + off + 128 * (idx % LT)
                        blk = src[:, at:at + 128]
                    elif idx < TOP:
                        blk = pair[:, idx - PAIR, :]
                    else:
                        blk = src[:, 128 * (idx - TOP):128 * (idx - TOP) + 128]
                    last = nc.tensor.transpose(o[:, size * k:size * (k + 1)], blk, ident[0:size, 0:size])
                last.then_inc(s_mf, 1)

            def scores(t):
                g = t // TPC
                b, k = t // (NT // B), g % 2
                cols = slice(128 * (t % TPC), 128 * (t % TPC + 1))
                pe.wait_ge(s_split, g + 1)
                if t % (NT // B) == 0:
                    pe.wait_ge(s_w[b], 1)
                if t:
                    pe.wait_ge(s_ex, t)
                pairs = ((mh, wh), (mh, wl), (ml, wh), (mr, wr))
                for n, (m, w) in enumerate(pairs):
                    for i in range(2):
                        last = nc.tensor.matmul(ps[:, i, 0:HALF], m[:, k, cols], w[b][:, HALF * i:HALF * (i + 1)],
                                                start=n == 0, stop=n == 3)
                last.then_inc(s_sc, 1)

            def transpose(t):
                k, j = t % 2, t % TPC
                pe.wait_ge(s_pn, t + 1)
                if t:
                    pe.wait_ge(s_el, t)
                if j == 0 and t:
                    pe.wait_ge(s_rl, 2 * (t // TPC))
                for i in range(LT):
                    nc.tensor.transpose(pt[:, i, :], p[:, k, 128 * i:128 * (i + 1)], ident[:, :])
                nc.tensor.transpose(pr[:, 128 * j:128 * (j + 1)], p[:, k, 128 * LT:L], ident[:, :]).then_inc(s_tr, 1)

            def tap_list(g):
                b, k = g // NCH, g % 2
                found = []
                def add(idx, blk, off, width, rows=128):
                    kk = [t[b][0:rows, idx, :] for t in (kh, kl)]
                    yy = [y[0:rows, k, hl, blk, off:off + width] for hl in range(2)]
                    found.append((kk[0], yy[0], width))
                    found.append((kk[0], yy[1], width))
                    found.append((kk[1], yy[0], width))
                for di in range(NDJ):
                    if di == 2:
                        add(PAIR, LT, 0, CHUNK)
                        if g % NCH == 0:
                            for i in range(LT + 1):
                                add(TOP + i, i, PADC, W, 128 if i < LT else LREM)
                    for i in range(LT):
                        add(LT * di + i, i, W * di, CHUNK)
                add(PAIR + 1, LT, PADC, CHUNK)
                return found

            def main(g, part, half):
                b, i = g // NCH, g % NCH
                if part == 0 and half == 0:
                    if i == 0:
                        wait_emptied(pe, "kc", b, 2)
                        pe.wait_ge(s_pad0, 3 * (b + 1))
                    else:
                        pe.wait_ge(s_hp, 3 * (g - b))
                    pe.wait_ge(s_rl, 2 * (g + 1))
                    if g >= 2:
                        pe.wait_ge(s_fin, 4 * (g - 1))
                work = tap_list(g)
                at_behind, at_last_behind = len(work) - 3 * (LT + 1), len(work) - 3
                sixth = 2 * part + half
                for n in range(len(work) * sixth // 6, len(work) * (sixth + 1) // 6):
                    lhs, rhs, width = work[n]
                    if n == at_behind:
                        pe.wait_ge(s_hn, 2 * g + 1)
                    if n == at_last_behind:
                        pe.wait_ge(s_hn, 2 * (g + 1))
                    last = nc.tensor.matmul(pa[:, g % 2, 0:width], lhs, rhs, start=n == 0, stop=n == len(work) - 1)
                if sixth == 5:
                    last.then_inc(s_mn, 1)

            def column_off(b, _):
                pe.wait_ge(s_yc, column_copies(NCH * (b + 1) - 1))
                o = misc("cc", b, 0)
                work = []
                for idx in range(NK):
                    if idx < PAIR:
                        rows, blk, at, width = 128, idx % LT, idx // LT, H
                    elif idx < TOP:
                        rows, blk, at, width = 128, LT, 2 * (idx - PAIR), H
                    else:
                        rows, blk, at, width = (128 if idx - TOP < LT else LREM), idx - TOP, H + 4, 2
                    for kk, hl in ((kch, 0), (kch, 1), (kcl, 0)):
                        work.append((kk[b][0:rows, idx, :], ycol[0:rows, b, hl, blk, at:at + width], width))
                for n, (lhs, rhs, width) in enumerate(work):
                    last = nc.tensor.matmul(o[0:C, 0:width], lhs, rhs, start=n == 0, stop=n == len(work) - 1)
                last.then_inc(s_mf, 1)

            def x1_turned(b, i):
                part = slice(64 + C * b, 64 + C * (b + 1))
                pe.wait_ge(s_xd[b], i + 1)
                o = misc("zn", b, i)
                for k in range(16):
                    at = W * (16 * i + k)
                    last = nc.tensor.transpose(o[0:W, C * k:C * (k + 1)], xd[part, at:at + W], ident[part, part])
                last.then_inc(s_mf, 1)

            def cosine_w(b, i):
                pe.wait_ge(s_cos, 16)
                wait_emptied(pe, "zn", b, 2)
                o = misc("d1", b, i)
                for k in range(8):
                    c = 16 * i + 2 * k
                    last = nc.tensor.matmul(o[0:2 * H, W * k:W * (k + 1)], zn[:, c:c + 2, :].rearrange("w c h -> w (c h)"),
                                            cosm[0:W, 0:W], start=True, stop=True)
                last.then_inc(s_mf, 1)

            def cosine_h(b, i):
                wait_emptied(pe, "d1", b, i)
                o = misc("d2", b, i)
                nc.tensor.matmul(o[0:2 * H, 0:CHUNK], cosm[:, :], d1[:, CHUNK * i:CHUNK * (i + 1)],
                                 start=True, stop=True).then_inc(s_mf, 1)

            handlers = {"conv2": conv2, "conv1": lambda b, i: conv("conv1", P_W1, b, i),
                        "conva": lambda b, i: conv("conva", P_WA, b, i), "norm": norm, "inorm": inverse_norms, "u": tap_sums,
                        "k": lambda b, i: tap_blocks("k", b, i), "kc": lambda b, i: tap_blocks("kc", b, i),
                        "cc": column_off, "zn": x1_turned, "d1": cosine_w, "d2": cosine_h}
            perform(before, handlers)
            scores(0)
            for s in range(steps):
                if s + 1 < NT:
                    scores(s + 1)
                g, part = divmod(s - LAG, TPC)
                perform(gaps.get((s, 0), []), handlers)
                if s >= LAG:
                    main(g, part, 0)
                perform(gaps.get((s, 1), []), handlers)
                if s >= LAG:
                    main(g, part, 1)
                perform(gaps.get((s, 2), []), handlers)
                if s < NT:
                    transpose(s)
            perform(behind, handlers)

        @block.scalar
        def _(act):
            def x_high(b, i):
                act.wait_ge(s_xn[b], i + 1)
                if b and i == 0:
                    act.wait_ge(s_mf, misc_no["conva", b - 1, NCH - 1] + 1)
                cols = slice(Q // 2 * i, Q // 2 * (i + 1))
                nc.scalar.activation(x3[:, cols], xn[:, cols], ACT.Copy).then_inc(s_x3h[b], 1)

            def residual(b, _):
                act.wait_ge(s_x[b], 16 * 4)
                act.wait_ge(s_bd6, 1)
                part = slice(64 + C * b, 64 + C * (b + 1))
                nc.scalar.activation(v2[part, :], v2[part, :], ACT.Identity, bias=bd6[part, 0:1]).then_inc(s_xres[b], 1)

            def conv_sums(name, b, i, width, which, scale=1.0):
                o = group(act, name, b, i)
                k = conv_no(name, b, i)
                if k == 0:
                    act.wait_ge(s_nb, 2)
                if k >= 2:
                    act.wait_ge(s_zf, k - 1)
                    if embed_splits(k - 2):
                        act.wait_ge(s_ef, embed_splits(k - 2))
                nc.scalar.activation(zneg[:, k % 2, 0:width], o[0:96, 0:width], ACT.Relu, bias=nbias[:, which:which + 1],
                                     scale=-scale).then_inc(s_zs, 1)
                nc.scalar.activation(z[:, k % 2, 0:width], o[0:96, 0:width], ACT.Relu,
                                     bias=par[0:96, P_B1 + which:P_B1 + which + 1], scale=scale).then_inc(s_free["act"], 1)

            def query_high(b, i):
                g = NCH * b + i
                k, cols = g % 2, slice(CHUNK * i, CHUNK * (i + 1))
                if i == 0:
                    act.wait_ge(s_mim[b], 16 * IM2COL)
                if g >= 2:
                    act.wait_ge(s_sc, TPC * (g - 1))
                nc.scalar.activation(mh[:, k, :], vim[:, cols], ACT.Copy).then_inc(s_splith, 1)
                nc.scalar.activation(mr[:, k, :], v2[0:48, cols], ACT.Copy).then_inc(s_splith, 1)

            def squares(b, _):
                act.wait_ge(s_wim[b], 16 * IM2COL)
                nc.scalar.activation(sq[:, :], wim[:, :], ACT.Square).then_inc(s_sq[b], 1)
                nc.scalar.activation(sq8[:, :], wim8[0:CR, :], ACT.Square).then_inc(s_sq[b], 1)

            def keys_high(b, _):
                wait_emptied(act, "inorm", b, 1)
                nc.scalar.activation(wh[b][:, :], wim[:, :], ACT.Copy).then_inc(s_whi[b], 1)
                nc.scalar.activation(wr[b][:, :], wim8[:, :], ACT.Copy).then_inc(s_whi[b], 1)

            def tap_sums(b, n):
                if b and n == 0:
                    act.wait_ge(s_mf, misc_no["kc", b - 1, 2] + 1)
                o = group(act, "u", b, n)
                dst = vc if n // 4 else v
                at = VROW * (BETA if n // 2 % 2 else ALPHA) + VHALF * (n % 2)
                rows = C if n // 4 else 128
                nc.scalar.activation(dst[:, at:at + VHALF], o[0:rows, 0:VHALF], ACT.Copy).then_inc(s_free["act"], 1)

            def taps_high(name, b, n):
                if b and name == "k" and n == 0:
                    act.wait_ge(s_mim[b], 16 * IM2COL)
                groups, dst, size = (K_GROUPS, kh[b], 128) if name == "k" else (KC_GROUPS, kch[b], C)
                blocks = groups[n]
                o = group(act, name, b, n)
                nc.scalar.activation(dst[:, blocks[0]:blocks[-1] + 1, :], grouped(o, blocks, size), ACT.Copy,
                                     scale=-1.0 if blocks[0] >= TOP else 1.0).then_inc(s_kh, 1)

            def exp(t):
                act.wait_ge(s_mx, t + 1)
                if t >= 2:
                    act.wait_ge(s_tr, t - 1)
                nc.scalar.activation(p[:, t % 2, :].rearrange("p (a c) -> p a c", a=2), ps[:, :, 0:HALF], ACT.Exp,
                                     bias=negm[:, t % 2:t % 2 + 1], accum_out=psm[:, t % 2:t % 2 + 1]).then_inc(s_ex, 1)

            def y_high(t):
                g, j, k = t // TPC, t % TPC, t // TPC % 2
                act.wait_ge(s_tr, t + 1)
                if j == 0 and g >= 2:
                    act.wait_ge(s_mn, g - 1)
                    act.wait_ge(s_hp, 3 * (g - 1 - (g - 1) // NCH))
                    act.wait_ge(s_yc, column_copies(g - 2))
                at = PADC + 128 * j
                nc.scalar.activation(y[:, k, 0, 0:LT, at:at + 128], pt[:, :, :], ACT.Copy).then_inc(s_eh, 1)
                if j == TPC - 1:
                    nc.scalar.activation(y[0:LREM, k, 0, LT, PADC:PADC + CHUNK], pr[:, 0:CHUNK], ACT.Copy).then_inc(s_rh, 1)
                    nc.scalar.activation(y[LREM:128, k, 0, LT, W:W + CHUNK], pr[:, 0:CHUNK], ACT.Copy).then_inc(s_rh, 1)

            def rows_before(g):
                k, n = g % 2, (g - 1) % 2
                act.wait_ge(s_el, TPC * g)
                act.wait_ge(s_rl, 2 * g)
                if g >= 2:
                    act.wait_ge(s_mn, g - 1)
                for rows, blocks, width in ((slice(0, 128), slice(0, LT), PADC), (slice(0, LREM), LT, PADC),
                                            (slice(LREM, 128), LT, W)):
                    nc.scalar.activation(y[rows, k, :, blocks, 0:width], F(y[rows, n, :, blocks, CHUNK:CHUNK + width]),
                                         ACT.Copy).then_inc(s_hp, 1)

            def x1_turned(b, i):
                if i == 0:
                    if b:
                        act.wait_ge(s_mf, misc_no["d1", b - 1, 1] + 1)
                    else:
                        place_free(act)
                o = group(act, "zn", b, i)
                nc.scalar.activation(zn[:, :, 16 * i:16 * (i + 1)], o[0:W, 0:512].rearrange("w (h c) -> w c h", c=C),
                                     ACT.Copy).then_inc(s_free["act"], 1)

            def cosine_w(b, i):
                if b and i == 0:
                    act.wait_ge(s_mf, misc_no["d2", b - 1, 1] + 1)
                o = group(act, "d1", b, i)
                nc.scalar.activation(d1[:, CHUNK * i:CHUNK * (i + 1)], o[0:2 * H, 0:CHUNK], ACT.Copy).then_inc(s_free["act"], 1)

            handlers = {"scale": x_high, "residual": residual,
                        "conv2": lambda b, i: conv_sums("conv2", b, i, HALF, 1, 0.25),
                        "conv1": lambda b, i: conv_sums("conv1", b, i, CHUNK, 0),
                        "conva": lambda b, i: conv_sums("conva", b, i, CHUNK, 2),
                        "squares": squares, "keys": keys_high, "split": query_high, "u": tap_sums,
                        "k": lambda b, i: taps_high("k", b, i), "kc": lambda b, i: taps_high("kc", b, i),
                        "zn": x1_turned, "d1": cosine_w}
            perform(before, handlers)
            exp(0)
            for s in range(steps):
                if s + 1 < NT:
                    exp(s + 1)
                if s < NT and s % TPC == 1 and s // TPC % NCH:
                    rows_before(s // TPC)
                for n in range(3):
                    perform(gaps.get((s, n), []), handlers)
                if s < NT:
                    y_high(s)
            perform(behind, handlers)

        @block.vector
        def _(dve):
            chain = [0]

            def link(ins):
                chain[0] += 1
                ins.then_inc(dve_chain, 1)
                dve.wait_ge(dve_chain, chain[0])

            def row_statistics(src, rows, stats, chunks):
                for i in chunks:
                    link(nc.vector.bn_stats(stats[rows, i, :], src[:, CHUNK * i:CHUNK * (i + 1)]))

            def deviation(rows, stats, m, var_ready, root_ready):
                link(nc.vector.bn_aggr(m[rows, 0:2], stats[rows, :, :]))
                nc.vector.tensor_scalar_add(m[rows, 1:2], m[rows, 1:2], GN_EPS).then_inc(var_ready, 1)
                dve.wait_ge(root_ready, 1)

            def statistics(b, i):
                dve.wait_ge(s_x[b], 16 * 4)
                row_statistics(xn, slice(0, 96), bnst, (2 * i, 2 * i + 1))

            def scale(b, i):
                if i == 0:
                    deviation(slice(0, 96), bnst, mv, s_var[b], s_root[b])
                cols = slice(Q // 2 * i, Q // 2 * (i + 1))
                nc.vector.tensor_scalar(xn[:, cols], xn[:, cols], mv[:, 0:1], mv[:, 3:4], ALU.subtract,
                                        ALU.mult).then_inc(s_xn[b], 1)

            def x_low(b, i):
                cols = slice(Q // 2 * i, Q // 2 * (i + 1))
                dve.wait_ge(s_xn[b], i + 1)
                dve.wait_ge(s_x3h[b], i + 1)
                nc.vector.tensor_tensor(x3[64:96, cols], xn[64:96, cols], F(x3[64:96, cols]), ALU.subtract).then_inc(s_x3[b], 1)

            def conv_weights():
                dve.wait_ge(s_par, 16)
                nc.vector.tensor_scalar_mul(bd6[64:128, :], par[64:128, P_BD:P_BD + 1], 1.0 / 6.0).then_inc(s_bd6, 1)
                nc.vector.tensor_scalar_mul(nbias[:, :], par[0:96, P_B1:P_B1 + 3], -1.0).then_inc(s_nb, 1)
                nc.vector.tensor_scalar_mul(nslope[:, :], par[0:96, P_A1:P_A1 + 3], -1.0).then_inc(s_nb, 1)
                link(nc.vector.tensor_copy(wst[:, :], par[0:96, 0:P_WD]))
                nc.vector.tensor_tensor(wst[32:64, :], par[32:64, 0:P_WD], F(wst[32:64, :]), ALU.subtract).then_inc(s_wst, 1)

            def prelu(name, b, i, which, dst, width):
                k = conv_no(name, b, i)
                if k == 0:
                    dve.wait_ge(s_nb, 2)
                wait_emptied(dve, name, b, i)
                if name == "conva":
                    shaped = [t.rearrange("p (i j) -> p i j", j=W) for t in (zneg[:, k % 2, :], z[:, k % 2, :])]
                    link(nc.vector.scalar_tensor_tensor(out=dst, in0=shaped[0], scalar=nslope[:, which:which + 1],
                                                        in1=shaped[1], op0=ALU.mult, op1=ALU.add))
                    nc.vector.scalar_tensor_tensor(out=z[64:96, k % 2, :], in0=zneg[64:96, k % 2, :],
                                                   scalar=nslope[64:96, which:which + 1], in1=z[64:96, k % 2, :],
                                                   op0=ALU.mult, op1=ALU.add).then_inc(s_zf, 1)
                else:
                    nc.vector.scalar_tensor_tensor(out=dst, in0=zneg[:, k % 2, 0:width], scalar=nslope[:, which:which + 1],
                                                   in1=z[:, k % 2, 0:width], op0=ALU.mult, op1=ALU.add).then_inc(s_zf, 1)
                dve.wait_ge(s_zf, k + 1)

            def edges(image, row, size, ready):
                link(nc.vector.memset(image[32:64, 2 * row:2 * row + size:row], 0.0))
                nc.vector.memset(image[64:96, row + 1:row + 1 + size:row], 0.0).then_inc(ready, 1)

            def ref_image(b, i):
                if b and i == 0:
                    dve.wait_ge(s_wim[b - 1], 16 * IM2COL)
                prelu("conv2", b, i, 1, wimg[:, WL + 1 + HALF * i:WL + 1 + HALF * (i + 1)], HALF)
                if i == 1:
                    edges(wimg, WL, L, s_wimg[b])

            def match_image(b, i):
                if b and i == 0:
                    dve.wait_ge(s_mim[b - 1], 16 * IM2COL)
                prelu("conv1", b, i, 0, mimg[:, W + 1 + CHUNK * i:W + 1 + CHUNK * (i + 1)], CHUNK)
                if i == NCH - 1:
                    edges(mimg, W, Q, s_mimg[b])

            def embed(b, i):
                if i == 0:
                    dve.wait_ge(s_x3h[b], 2)
                prelu("conva", b, i, 2, e3v[:, 2 + ROWS * i:2 + ROWS * (i + 1), 2:2 + W], CHUNK)

            def squares_joined(b, _):
                dve.wait_ge(s_sq[b], 2)
                nc.vector.tensor_tensor(sq[0:CR, :], sq[0:CR, :], sq8[:, :], ALU.add).then_inc(s_sqs[b], 1)

            def norms(b, _):
                o = group(dve, "norm", b, 0)
                nc.vector.tensor_scalar_max(nrm[:, 0:6], o[0:96, 0:6], NORM_EPS ** 2).then_inc(s_free["dve"], 1)

            def keys_scaled(b, i):
                o = group(dve, "inorm", b, i)
                cols = slice(HALF * i, HALF * (i + 1))
                link(nc.vector.scalar_tensor_tensor(out=wim8[:, cols], in0=wim8[:, cols], scalar=SOFTMAX_SCALE,
                                                    in1=o[0:48, 0:HALF], op0=ALU.mult, op1=ALU.mult))
                nc.vector.scalar_tensor_tensor(out=wim[:, cols], in0=wim[:, cols], scalar=SOFTMAX_SCALE,
                                               in1=o[:, 0:HALF], op0=ALU.mult, op1=ALU.mult).then_inc(s_free["dve"], 1)

            def keys_low(b, _):
                wait_emptied(dve, "inorm", b, 1)
                dve.wait_ge(s_whi[b], 2)
                link(nc.vector.tensor_tensor(wl[b][:, :], wim[:, :], F(wh[b][:, :]), ALU.subtract))
                link(nc.vector.tensor_tensor(wr[b][0:32, :], wim8[0:32, :], F(wr[b][0:32, :]), ALU.subtract))
                nc.vector.tensor_copy(wr[b][0:CR, :], wim8[0:CR, :]).then_inc(s_w[b], 1)

            def tap_sums(b, n):
                wait_emptied(dve, "u", b, 7)
                src, pair = ((v, vp), (vc, vcp))[n]
                link(nc.vector.tensor_tensor(src[:, VROW * FULL:VROW * FULL + VROW - WL], src[:, 0:VROW - WL],
                                             src[:, VROW * BETA + WL:VROW * (BETA + 1)], ALU.add))
                for di in range(NDJ):
                    kind, off = TAP_SRC[di]
                    at = VROW * kind + off + 128 * LT
                    nc.vector.tensor_copy(pair[:, di // 2, LREM * (di % 2):LREM * (di % 2 + 1)],
                                          src[:, at:at + LREM]).then_inc(s_vf[b], 1)

            def taps_low(name, b, n):
                groups, high, low, size = (K_GROUPS, kh[b], kl[b], 128) if name == "k" else (KC_GROUPS, kch[b], kcl[b], C)
                blocks = groups[n]
                o = group(dve, name, b, n)
                dve.wait_ge(s_kh, 10 * b + n + 1 + (7 if name == "kc" else 0))
                cols = slice(blocks[0], blocks[-1] + 1)
                nc.vector.scalar_tensor_tensor(out=low[:, cols, :], in0=grouped(o, blocks, size),
                                               scalar=-1.0 if blocks[0] >= TOP else 1.0, in1=F(high[:, cols, :]),
                                               op0=ALU.mult, op1=ALU.subtract).then_inc(s_free["dve"], 1)

            def maximum(t):
                dve.wait_ge(s_sc, t + 1)
                nc.vector.tensor_reduce(negm[:, t % 2:t % 2 + 1], ps[:, :, 0:HALF], AX.XY, ALU.max, negate=True).then_inc(s_mx, 1)

            def softmax(t):
                k = t % 2
                dve.wait_ge(s_ex, t + 1)
                link(nc.vector.reciprocal(rps[:, k:k + 1], psm[:, k:k + 1]))
                nc.vector.tensor_scalar_mul(p[:, k, :], p[:, k, :], rps[:, k:k + 1]).then_inc(s_pn, 1)

            def y_low(t):
                g, j, k = t // TPC, t % TPC, t // TPC % 2
                dve.wait_ge(s_eh, t + 1)
                at = PADC + 128 * j
                nc.vector.tensor_tensor(y[:, k, 1, 0:LT, at:at + 128], pt[:, :, :], F(y[:, k, 0, 0:LT, at:at + 128]),
                                        ALU.subtract).then_inc(s_el, 1)
                if j == TPC - 1:
                    dve.wait_ge(s_rh, 2 * (g + 1))
                    high = F(y[0:LREM, k, 0, LT, PADC:PADC + CHUNK])
                    nc.vector.tensor_tensor(y[0:LREM, k, 1, LT, PADC:PADC + CHUNK], pr[:, 0:CHUNK], high,
                                            ALU.subtract).then_inc(s_rl, 1)
                    nc.vector.tensor_tensor(y[LREM:128, k, 1, LT, W:W + CHUNK], pr[:, 0:CHUNK], high,
                                            ALU.subtract).then_inc(s_rl, 1)

            def finish(g, n):
                b, i = g // NCH, g % NCH
                if n == 0:
                    dve.wait_ge(s_mn, g + 1)
                    if i == 0:
                        dve.wait_ge(s_xres[b], 1)
                dj = (0, -2, -1, 1)[n]
                rows = x1(b)[:, CHUNK * i:CHUNK * (i + 1)].rearrange("c (i j) -> c i j", j=W)
                k = C * (dj + 2)
                acc = pa[k:k + C, g % 2, 0:CHUNK].rearrange("c (i j) -> c i j", j=W)
                lo, hi = max(0, -dj), W - max(0, dj)
                nc.vector.scalar_tensor_tensor(out=rows[:, :, lo:hi], in0=acc[:, :, lo + dj:hi + dj], scalar=1.0 / 6.0,
                                               in1=rows[:, :, lo:hi], op0=ALU.mult, op1=ALU.add).then_inc(s_fin, 1)
                dve.wait_ge(s_fin, 4 * g + n + 1)

            def column_off(b, _):
                dve.wait_ge(s_fin, 4 * (NCH * (b + 1) - 1))
                o = group(dve, "cc", b, 0)
                col = x1(b)[:, 0:Q:W]
                nc.vector.scalar_tensor_tensor(out=col, in0=o[0:C, 0:H], scalar=-1.0 / 6.0, in1=col, op0=ALU.mult,
                                               op1=ALU.add).then_inc(s_free["dve"], 1)
                wait_emptied(dve, "cc", b, 0)

            def x1_rows(b):
                return slice(64 + C * b, 64 + C * (b + 1))

            def x1_statistics(b, _):
                row_statistics(x1(b), x1_rows(b), bnst2, range(NCH - 1))

            def x1_deviation(b, _):
                row_statistics(x1(b), x1_rows(b), bnst2, (NCH - 1,))
                deviation(x1_rows(b), bnst2, mv2, s_var2[b], s_root2[b])

            def x1_normalise(b, i):
                if i == 0:
                    if b:
                        dve.wait_ge(s_mf, misc_no["zn", b - 1, 2] + 1)
                    else:
                        place_free(dve)
                rows, cols = x1_rows(b), slice(Q // 3 * i, Q // 3 * (i + 1))
                nc.vector.tensor_scalar(xd[rows, cols], x1(b)[:, cols], mv2[rows, 0:1], mv2[rows, 3:4], ALU.subtract,
                                        ALU.mult).then_inc(s_xd[b], 1)

            def result(b, i):
                if i == 0:
                    dve.wait_ge(s_xr[b], 16 * 2)
                    if b:
                        dve.wait_ge(s_out, 16 * 4 * b)
                    else:
                        place_free(dve)
                o = group(dve, "d2", b, i)
                cols = slice(CHUNK * i, CHUNK * (i + 1))
                nc.vector.tensor_tensor(res[:, cols], o[0:2 * H, 0:CHUNK], xr[:, cols], ALU.add).then_inc(s_free["dve"], 1)

            handlers = {"rows": statistics, "scale": scale, "low": x_low, "conv2": ref_image, "conv1": match_image, "conva": embed, "squares": squares_joined, "norm": norms, "inorm": keys_scaled,
                        "keys": keys_low, "sums": tap_sums, "k": lambda b, i: taps_low("k", b, i), "kc": lambda b, i: taps_low("kc", b, i),
                        "cc": column_off, "stats": x1_statistics, "deviation": x1_deviation, "x1n": x1_normalise,
                        "d2": result}
            conv_weights()
            perform(before, handlers)
            maximum(0)
            softmax(0)
            for s in range(steps):
                if s + 1 < NT:
                    maximum(s + 1)
                if s + 1 < NT:
                    softmax(s + 1)
                for n in range(3):
                    g, tap = divmod(3 * (s - LAG - TPC) + n - 1, 3 * TPC)
                    if g >= 0 and tap < NDJ:
                        finish(g, tap)
                    perform(gaps.get((s, n), []), handlers)
                if s < NT:
                    y_low(s)
            for n in range(NDJ):
                finish(NG - 1, n)
            perform(behind, handlers)


def kernel(**inputs):
    import concourse.bacc as bacc
    from concourse.bass_utils import run_bass_kernel_spmd

    a = {k.replace("L0_conv_", ""): np.asarray(v) for k, v in inputs.items()}
    par = np.zeros((128, NP), np.float32)
    w1t, w2t, wat = a["W1"].T, a["W2"].T, a["Wa"].T
    wdt = a["Wd"].transpose(1, 2, 3, 0).reshape(C, 9 * C)
    for r in range(3):
        rows = slice(32 * r, 32 * (r + 1))
        for k in range(3):
            par[rows, P_W1 + 32 * k:P_W1 + 32 * k + CR] = w1t
            par[rows, P_W2 + 32 * k:P_W2 + 32 * k + CR] = w2t
            par[rows, P_WA + 32 * k:P_WA + 32 * (k + 1)] = wat
        par[rows, P_WD:P_B1] = wdt
        par[32 * r:32 * r + CR, P_B1] = a["b1"]
        par[32 * r:32 * r + CR, P_B2] = a["b2"]
        par[rows, P_BA] = a["ba"]
    par[:, P_A1], par[:, P_A2], par[:, P_AA] = a["a1"][0], a["a2"][0], a["aa"][0]
    for b in range(B):
        par[64 + C * b:64 + C * (b + 1), P_BD] = a["bd"]
    k, n = np.arange(W)[:, None], np.arange(W)[None, :]
    dct = np.cos(np.pi * (2.0 * n + 1.0) * k / (2.0 * W)) * np.where(k == 0, np.sqrt(1.0 / W), np.sqrt(2.0 / W))
    arrays = {"x": np.ascontiguousarray(a["x"]), "params": par, "dct": np.kron(np.eye(2), dct.T).astype(np.float32)}

    nc = bacc.Bacc("TRN2", target_bir_lowering=False, num_devices=1)
    ins = [nc.dram_tensor(n, v.shape, F32, kind="ExternalInput").ap() for n, v in arrays.items()]
    out = nc.dram_tensor("out", (B, C, H, W), F32, kind="ExternalOutput").ap()
    x1_copy = nc.dram_tensor("x1_copy", (B, C, H * W), F32, kind="Internal").ap()
    program(nc, *ins, x1_copy, out)
    return run_bass_kernel_spmd(nc, [arrays], core_ids=[0]).results[0]["out"]
```

```python
from contextlib import ExitStack

import concourse.bass as bass
import concourse.mybir as mybir
import numpy as np

F32 = mybir.dt.float32
F32R = mybir.dt.float32r
ALU = mybir.AluOpType
ACT = mybir.ActivationFunctionType
AX = mybir.AxisListType

B, C, H, W = 2, 32, 48, 48
CR = C // 2
Q = H * W
HL, WL = H // 2, W // 2
L = HL * WL
HALF = L // 2
ROWS = 8
CHUNK = ROWS * W
NCH = Q // CHUNK
TPC = CHUNK // 128
NT = B * Q // 128
NG = B * NCH
LT = L // 128
LREM = L - 128 * LT
X_FIRST = 2 * CHUNK
PADC = 2 * W
WIN = PADC + CHUNK + W
NDJ = 4
MY = HL + 2
VROW = MY * WL
VHALF = VROW // 2
EW = W + 4
GN_EPS = 1e-5
NORM_EPS = 1e-4
SOFTMAX_SCALE = 10.0
LAG = 4

ZBUF = 3
NK = 4 * LT + 2 + LT + 1
PAIR, TOP = 4 * LT, 4 * LT + 2
ALPHA, FULL, BETA = 0, 1, 2
TAP_SRC = [(ALPHA, 2 * WL), (FULL, WL), (FULL, 0), (BETA, 0)]

P_W1, P_W2, P_WA, P_WD = 0, 96, 192, 288
P_B1, P_B2, P_BA, P_A1, P_A2, P_AA, P_BD = 576, 577, 578, 579, 580, 581, 582
NP = 584

SHIFTS = [(0, 3), (-1, 3), (1, 2)]
IM2COL = len(SHIFTS) + 3


EMPTIES = {"conv2": "act", "conv1": "act", "conva": "act", "norm": "dve", "inorm": "dve", "u": "act", "k": "dve",
           "kc": "dve", "cc": "dve", "zn": "act", "d1": "dve", "d2": "dve"}


BEFORE = [
    ("rows", (0, 1, 2)), ("scale", (0, 1)), ("low", (0, 1)), ("conv2", (0, 1)), ("conv1", (0, 1, 2, 3, 4, 5)),
    ("squares", (0,)), ("conva", (0, 1)), ("norm", (0,)), ("conva", (2,)), ("split", (0,)), ("inorm", (0,)),
    ("conva", (3,)), ("inorm", (1,)), ("conva", (4,)), ("keys", (0,)), ("conva", (5,)), ("split", (1,))]
SPREAD = [
    ("u", 0, 8, 2, 0.5), ("sums", 0, 2, 4, 0.5), ("k", 0, 7, 6, 0.5), ("kc", 0, 3, 9, 0.5), ("residual", 0, 1, 7, 1),
    ("rows", 1, 3, 6, 1.5), ("scale", 1, 2, 11, 1), ("low", 1, 2, 12, 1), ("conv2", 1, 2, 15, 1),
    ("conv1", 1, NCH, 22, 1), ("conva", 1, NCH, 28, 1.5), ("squares", 1, 1, 28, 1), ("norm", 1, 1, 30, 1),
    ("inorm", 1, 2, 37, 0.5), ("keys", 1, 1, 43, 1), ("u", 1, 8, 40, 1), ("sums", 1, 2, 46, 1), ("k", 1, 7, 50, 1),
    ("kc", 1, 3, 59, 0.5), ("residual", 1, 1, 62, 1), ("cc", 0, 1, 60, 1), ("stats", 0, 4, 63, 1),
    ("stats", 0, 1, 67, 1), ("deviation", 0, 1, 75, 1), ("x1n", 0, 3, 79, 3), ("zn", 0, 3, 91, 0.5),
    ("cc", 1, 1, 113, 1), ("stats", 1, 4, 116, 1), ("stats", 1, 1, 119, 1)]
SPLIT_LEAD = 7
FINISH_GAP = 0


def stages(b, *names):
    return [(name, b, i) for name, n in names for i in range(n)]


def side_jobs():
    before = [(name, 0, k) for name, parts in BEFORE for k in parts]
    gaps = {}
    parts = {}
    for name, b, n, first, pace in SPREAD:
        for k in range(n):
            part = parts[name, b] = parts.get((name, b), -1) + 1
            gaps.setdefault(divmod(first + int(k * pace), 3), []).append((name, b, part))
    for g in range(2, NG):
        gaps.setdefault(divmod(3 * TPC * g - SPLIT_LEAD, 3), []).append(("split", g // NCH, g % NCH))
    behind = (stages(1, ("deviation", 1)) + stages(0, ("d1", 2)) + stages(1, ("x1n", 3), ("zn", 3))
              + stages(0, ("d2", 2)) + stages(1, ("d1", 2), ("d2", 2)))
    ordered = before + [job for at in sorted(gaps) for job in gaps[at]] + behind
    assert max(gaps)[0] < NT + LAG
    for b in range(B):
        places = {name: [ordered.index(job) for job in ordered if job[:2] == (name, b)] for name, _, _ in ordered}
        assert all(p == sorted(p) for p in places.values())
        assert places["rows"][-1] < places["scale"][0]
    return before, gaps, behind


def conv_no(name, b, i):
    return (2 + 2 * NCH) * b + {"conv2": 0, "conv1": 2, "conva": 2 + NCH}[name] + i


def embed_splits(k):
    b, i = k // (2 + 2 * NCH), k % (2 + 2 * NCH) - (2 + NCH)
    return NCH * b + i + 1 if i >= 0 else 0


def column_copies(g):
    return 6 * (g + 1) + 4 * (g // NCH + 1)


def grouped(bank, blocks, size):
    return bank[:, 0:size * len(blocks)].rearrange("p (n c) -> p n c", c=size)


K_GROUPS = [range(4 * n, 4 * n + 4) for n in range(4)] + [range(PAIR, TOP), range(TOP, TOP + 4), range(TOP + 4, NK)]
KC_GROUPS = [range(0, PAIR), range(PAIR, TOP), range(TOP, NK)]


def program(nc, x, params, dct, x1_copy, out):
    before, gaps, behind = side_jobs()
    steps = NT + LAG
    ordered = before + [job for s in range(steps) for n in range(3) for job in gaps.get((s, n), [])] + behind
    plan = [job for job in ordered if job[0] in EMPTIES]
    misc_no = {job: n for n, job in enumerate(plan)}

    def emptied(n):
        eng = EMPTIES[plan[n][0]]
        return eng, sum(EMPTIES[name] == eng for name, _, _ in plan[:n + 1])

    with ExitStack() as ctx:
        def sb(name, shape, dt=F32):
            return ctx.enter_context(nc.sbuf_tensor(name, shape, dt))

        def pb(name, shape):
            return ctx.enter_context(nc.psum_tensor(name, shape, F32))

        def sem(name):
            return ctx.enter_context(nc.semaphore(name))

        def sems(name, n=B):
            return [sem(f"{name}{i}") for i in range(n)]

        ident = sb("ident", [128, 128])
        ones = sb("ones", [128, 128])
        par = sb("par", [128, NP])
        wst = sb("wst", [96, P_WD], F32R)
        cosm = sb("cosm", [2 * W, 2 * W])
        cosh = sb("cosh", [2 * W, 2 * W], F32R)
        cosl = sb("cosl", [2 * W, 2 * W], F32R)
        nbias = sb("nbias", [96, 3])
        nslope = sb("nslope", [96, 3])
        mhalf = sb("mhalf", [128, 1])
        bd6 = sb("bd6", [128, 1])
        bnst = sb("bnst", [96, NCH, 6])
        bnst2 = sb("bnst2", [128, NCH, 6])
        mv2 = sb("mv2", [128, 4])
        mv = sb("mv", [96, 4])
        y = sb("y", [128, 2, 2, LT + 1, WIN], F32R)
        ycol = sb("ycol", [128, B, 2, LT + 1, H + 6], F32R)
        kh = [sb("kh0", [128, NK, 128], F32R)]
        kl = [sb("kl0", [128, NK, 128], F32R)]
        kch = [sb(f"kch{b}", [128, NK, C], F32R) for b in range(B)]
        kcl = [sb(f"kcl{b}", [128, NK, C], F32R) for b in range(B)]
        vim = sb("vim", [128, Q])
        v2 = sb("v2", [128, Q])
        p = sb("p", [128, 2, L])
        mh = sb("mh", [128, 2, CHUNK], F32R)
        ml = sb("ml", [128, 2, CHUNK], F32R)
        mr = sb("mr", [48, 2, CHUNK], F32R)
        wh = [sb(f"wh{b}", [128, L], F32R) for b in range(B)]
        wl = [sb(f"wl{b}", [128, L], F32R) for b in range(B)]
        wr = [sb(f"wr{b}", [48, L], F32R) for b in range(B)]
        negm = sb("negm", [128, 2])
        psm = sb("psm", [128, 2])
        rps = sb("rps", [128, 2])
        z = sb("z", [96, ZBUF, CHUNK])
        zneg = sb("zneg", [96, 2, CHUNK])
        with ExitStack() as over:
            kh.append(over.enter_context(nc.sbuf_tensor("kh1", [128, NK, 128], F32R)))
            kl.append(over.enter_context(nc.sbuf_tensor("kl1", [128, NK, 128], F32R)))
        with ExitStack() as over:
            xn = over.enter_context(nc.sbuf_tensor("xn", [96, Q], F32))
        e3 = sb("e3", [96, EW * EW], F32R)
        x3 = sb("x3", [96, Q], F32R)
        mimg = sb("mimg", [96, Q + 2 * (W + 1)])
        with ExitStack() as over:
            xd = over.enter_context(nc.sbuf_tensor("xd", [128, Q], F32))
            zn = over.enter_context(nc.sbuf_tensor("zn", [W, C, H], F32))
            xr = [over.enter_context(nc.sbuf_tensor(f"xr{b}", [2 * H, C // 2 * W], F32)) for b in range(B)]
            d1h = over.enter_context(nc.sbuf_tensor("d1h", [2 * H, C // 2 * W], F32R))
            d1l = over.enter_context(nc.sbuf_tensor("d1l", [2 * H, C // 2 * W], F32R))
            res = [over.enter_context(nc.sbuf_tensor(f"res{b}", [2 * H, C // 2 * W], F32)) for b in range(B)]
        wimg = sb("wimg", [96, L + 2 * (WL + 1)])
        wim = sb("wim", [128, L])
        wim8 = sb("wim8", [48, L])
        sq = sb("sq", [128, L])
        sq8 = sb("sq8", [CR, L])
        nrm = sb("nrm", [96, 12])
        v = sb("v", [128, 3 * VROW])
        vc = sb("vc", [C, 3 * VROW])
        vp = sb("vp", [128, 2, 128])
        vcp = sb("vcp", [C, 2, 128])
        ww = sb("ww", [96, 3, 6, 128], F32R)

        ps = pb("ps", [128, 2, 512])
        pt = pb("pt", [128, LT, 128])
        pr = pb("pr", [LREM, 512])
        pa = pb("pa", [128, 2, 512])
        pm = pb("pm", [128, 2, 512])

        s_par = sem("params_in")
        s_cos = sem("cos_in")
        s_cosl = sem("cos_split")
        s_d1h = sem("cosine_w_high")
        s_x0 = sems("x_first_part_in")
        s_x = sems("x_in")
        s_xin = sems("residual_x_in")
        s_mim = sems("match_im2col_in")
        s_wim = sems("ref_im2col_in")
        s_out = sem("stored")
        s_const = sem("constants")
        s_bd6 = sem("output_bias")
        dve_chain = sem("dve_chain")
        pool_chain = sem("pool_chain")
        s_wst = sem("conv_weights_split")
        s_ww = sem("tap_weights_laid")
        s_var = sems("variance")
        s_root = sems("inverse_root")
        s_xn = sems("xn_ready")
        s_x3h = sems("x3_high")
        s_x3 = sems("x3_ready")
        s_xres = sems("x_plus_bias")
        s_mf = sem("misc_full")
        s_free = {"act": sem("misc_emptied_act"), "dve": sem("misc_emptied_dve")}
        s_zf = sem("prelu_done")
        s_ef = sem("embed_split")
        s_wimg = sems("ref_image")
        s_mimg = sems("match_image")
        s_epad = sems("embed_padding")
        s_sq = sems("squares")
        s_sqs = sems("squares_joined")
        s_inv = sems("inverse_norms")
        s_whi = sems("keys_high")
        s_w = sems("keys_ready")
        s_vf = sems("tap_sums_ready")
        s_kh = sem("tap_high")
        s_splith = sem("query_high")
        s_split = sem("query_split")
        s_sc = sem("scores")
        s_mx = sem("max")
        s_ex = sem("exp")
        s_rec = sem("inverse_sum")
        s_pn = sem("softmax")
        s_tr = sem("transposed")
        s_eh = sem("y_high")
        s_el = sem("y_low")
        s_rh = sem("y_last_high")
        s_rl = sem("y_last_low")
        s_pad0 = sem("window_padding")
        s_hn = sem("row_behind_copied")
        s_hp = sem("rows_before_copied")
        s_yc = sem("column_copied")
        s_mn = sem("taps_done")
        s_fin = sem("x1_chunk")
        s_var2 = sems("variance2")
        s_root2 = sems("inverse_root2")
        s_x1out = sems("x1_stored")
        s_xr = sems("residual_in")
        s_nb = sem("negative_constants")
        s_xd = sems("x1_normalised")

        block = ctx.enter_context(nc.Block())

        def F(ap):
            return ap.bitcast(F32)

        def wait_emptied(eng, name, b, i):
            who, count = emptied(misc_no[name, b, i])
            eng.wait_ge(s_free[who], count)

        def group(eng, name, b, i):
            n = misc_no[name, b, i]
            eng.wait_ge(s_mf, n + 1)
            return pm[:, n % 2, :]

        x3v = x3[:, :].rearrange("p (i s j u) -> p i s j u", s=2, j=WL, u=2)
        e3v = e3[:, :].rearrange("p (i j) -> p i j", j=EW)
        e3f = F(e3[:, :])

        def place_free(eng):
            eng.wait_ge(s_mf, misc_no["kc", B - 1, 2] + 1)
            eng.wait_ge(s_wim[B - 1], 16 * IM2COL)

        def perform(jobs, handlers):
            for name, b, i in jobs:
                if name in handlers:
                    handlers[name](b, i)

        def x1(b):
            return v2[64 + C * b:64 + C * (b + 1), :]

        @block.sync
        def _(sp):
            def load_x(b):
                if b:
                    sp.wait_ge(s_mf, misc_no["u", b - 1, 7] + 1)
                src = x[b].rearrange("c h w -> c (h w)")
                for part, arrived in ((slice(0, X_FIRST), s_x0[b]), (slice(X_FIRST, Q), s_x[b])):
                    for r in range(3):
                        sp.dma_start(xn[C * r:C * (r + 1), part], src[:, part]).then_inc(arrived, 16)

            def im2col(b, image, ready, row, size, full, last, done):
                sp.wait_ge(s_const, 6)
                sp.wait_ge(ready, 1)
                pitch = image.shape[1]
                for k, (dx, n) in enumerate(SHIFTS):
                    src = image[32 * k:32 * k + CR, 1 + dx:1 + dx + size]
                    src = bass.AP(src.tensor, src.offset, [[pitch, CR], [row, n], [1, size]])
                    dst = full[3 * CR * k:3 * CR * k + n * CR, :]
                    sp.dma_start(dst, src).then_inc(done, 16)
                at = 2 * row + 1 + SHIFTS[2][0]
                src = image[64:64 + CR, at:at + size]
                for n in range(3):
                    sp.dma_start(last[CR * n:CR * (n + 1), :], src).then_inc(done, 16)

            for b in range(B):
                load_x(b)
                if not b:
                    sp.dma_start(par[:, :], params).then_inc(s_par, 16)
                sp.dma_start(x1(b), x[b].rearrange("c h w -> c (h w)")).then_inc(s_xin[b], 16)
                if not b:
                    sp.dma_start(cosm[:, :], dct).then_inc(s_cos, 16)
                if b:
                    sp.wait_ge(s_w[b - 1], 1)
                im2col(b, wimg, s_wimg[b], WL, L, wim, wim8, s_wim[b])
                if b:
                    sp.wait_ge(s_split, NCH * b)
                im2col(b, mimg, s_mimg[b], W, Q, vim, v2, s_mim[b])
            for b in range(B):
                sp.wait_ge(s_fin, 4 * NCH * (b + 1))
                wait_emptied(sp, "cc", b, 0)
                sp.dma_start(x1_copy[b], x1(b)).then_inc(s_x1out[b], 16)
                sp.wait_ge(s_x1out[b], 16)
                place_free(sp)
                pairs = x1_copy[b].rearrange("(p t) (h w) -> t h p w", t=2, w=W)
                for t in range(2):
                    dst = xr[b][H * t:H * (t + 1), :].rearrange("h (p w) -> h p w", w=W)
                    sp.dma_start(dst, pairs[t]).then_inc(s_xr[b], 16)
            for b in range(B):
                for i in range(2):
                    wait_emptied(sp, "d2", b, i)
                    dst = out[b].rearrange("(g p t) k l -> g t k p l", g=2, t=2)
                    for t in range(2):
                        sp.dma_start(dst[i, t], res[b][H * t:H * (t + 1), CHUNK * i:CHUNK * (i + 1)]
                                     .rearrange("k (p l) -> k p l", l=W)).then_inc(s_out, 16)
            sp.wait_ge(s_out, 16 * 4 * B)

        @block.gpsimd
        def _(pool):
            chain = [0]

            def link(ins):
                chain[0] += 1
                ins.then_inc(pool_chain, 1)
                pool.wait_ge(pool_chain, chain[0])

            link(pool.memset(ident[:, :], 0.0))
            pool.affine_select(out=ident[:, :], in_=ident[:, :], compare_op=ALU.not_equal, fill=1.0, base=0,
                               pattern=[[-1, 128]], channel_multiplier=1).then_inc(s_const, 1)
            pool.memset(ones[:, :], 1.0).then_inc(s_const, 1)
            link(pool.memset(mhalf[:, :], -0.5))
            link(pool.memset(F(ycol[:, :, :, :, :]), 0.0))
            link(pool.memset(F(ww[:, :, :, :]), 0.0))
            pool.memset(mimg[:, 0:W + 1], 0.0).then_inc(s_const, 1)
            pool.memset(mimg[:, W + 1 + Q:], 0.0).then_inc(s_const, 1)
            pool.memset(wimg[:, 0:WL + 1], 0.0).then_inc(s_const, 1)
            pool.memset(wimg[:, WL + 1 + L:], 0.0).then_inc(s_const, 1)

            def inverse_root(m, half, var_ready, ready):
                pool.wait_ge(var_ready, 1)
                pool.tensor_tensor(m[:, 3:4], m[:, 1:2], half, ALU.pow).then_inc(ready, 1)
                pool.wait_ge(ready, 1)

            def tap_weights():
                pool.wait_ge(s_par, 16)
                wd = par[0:96, P_WD:P_B1].rearrange("c (a b o) -> c a b o", a=3, b=3)
                places = ((0, 5, 0, 1), (1, 3, 0, 3), (2, 1, 0, 3), (3, 0, 1, 2))
                for dj, kx, b0, n in places:
                    link(pool.tensor_copy(ww[:, :, kx:kx + n, C * dj:C * (dj + 1)], wd[:, :, b0:b0 + n, :]))
                for dj, kx, b0, n in places:
                    dst = ww[32:64, :, kx:kx + n, C * dj:C * (dj + 1)]
                    pool.tensor_tensor(dst, wd[32:64, :, b0:b0 + n, :], F(dst), ALU.subtract).then_inc(s_ww, 1)
                pool.wait_ge(s_ww, 4)

            def scale(b, i):
                if i == 0:
                    inverse_root(mv[:, :], mhalf[0:96, :], s_var[b], s_root[b])

            def embed_padding(b, i):
                if i == 0:
                    return
                pool.wait_ge(s_x3[b], 2)
                pool.wait_ge(s_x3h[b], 2)
                pool.memset(e3f[:, 0:2 * EW + 2], 0.0).then_inc(s_epad[b], 1)
                pool.memset(e3f[:, (EW - 2) * EW - 2:], 0.0).then_inc(s_epad[b], 1)
                sides = e3f[:, 2 * EW + 50:2 * EW + 50 + EW * (H - 1)].rearrange("p (i j) -> p i j", j=EW)[:, :, 0:4]
                pool.memset(sides, 0.0).then_inc(s_epad[b], 1)
                pool.wait_ge(s_epad[b], 3)

            def embed_low(b, i):
                k = conv_no("conva", b, i)
                rows = e3v[64:96, 2 + ROWS * i:2 + ROWS * (i + 1), 2:2 + W]
                pool.wait_ge(s_zf, k + 1)
                pool.tensor_tensor(rows, z[64:96, k % ZBUF, :].rearrange("p (i j) -> p i j", j=W), F(rows),
                                   ALU.subtract).then_inc(s_ef, 1)
                pool.wait_ge(s_ef, NCH * b + i + 1)

            def inverse_norms(b, _):
                wait_emptied(pool, "norm", b, 0)
                pool.tensor_tensor(nrm[:, 6:12], nrm[:, 0:6], mhalf[0:96, 0:1].to_broadcast([96, 6]),
                                   ALU.pow).then_inc(s_inv[b], 1)
                pool.wait_ge(s_inv[b], 1)

            def query_low(b, i):
                g = NCH * b + i
                k = g % 2
                cols = slice(CHUNK * i, CHUNK * (i + 1))
                pool.wait_ge(s_splith, 2 * g + 1)
                link(pool.tensor_tensor(ml[:, k, :], vim[:, cols], F(mh[:, k, :]), ALU.subtract))
                pool.wait_ge(s_splith, 2 * g + 2)
                pool.tensor_tensor(mr[32:48, k, :], v2[32:48, cols], F(mr[32:48, k, :]), ALU.subtract).then_inc(s_split, 1)
                pool.wait_ge(s_split, g + 1)

            def first_padding(g):
                k = g % 2
                if g >= 2:
                    pool.wait_ge(s_mn, g - 1)
                counted(pool.memset(F(y[:, k, :, 0:LT, 0:PADC]), 0.0), "pad0", s_pad0)
                counted(pool.memset(F(y[0:LREM, k, :, LT, 0:PADC]), 0.0), "pad0", s_pad0)
                counted(pool.memset(F(y[LREM:128, k, :, LT, 0:W]), 0.0), "pad0", s_pad0)

            def last_padding(g):
                counted(pool.memset(F(y[:, g % 2, :, 0:LT, PADC + CHUNK:]), 0.0), "hn", s_hn)
                counted(pool.memset(F(y[LREM:128, g % 2, :, LT, W + CHUNK:WIN - W]), 0.0), "hn", s_hn)

            def row_behind(g):
                k, n = g % 2, (g + 1) % 2
                counted(pool.tensor_copy(y[:, k, :, 0:LT, PADC + CHUNK:], F(y[:, n, :, 0:LT, PADC:PADC + W])), "hn", s_hn)

            def row_behind_last(g):
                k, n = g % 2, (g + 1) % 2
                counted(pool.tensor_copy(y[LREM:128, k, :, LT, W + CHUNK:WIN - W], F(y[LREM:128, n, :, LT, W:2 * W])),
                        "hn", s_hn)

            def column(g):
                b, i, k = g // NCH, g % NCH, g % 2
                for rows, blocks, at, to in ((slice(0, 128), slice(0, LT), PADC, 2),
                                             (slice(0, LREM), slice(LT, LT + 1), PADC, 2),
                                             (slice(LREM, 128), slice(LT, LT + 1), W, 1)):
                    for hl in range(2):
                        src = F(y[rows, k, hl, blocks, at:at + CHUNK:W])
                        dst = ycol[rows, b, hl, blocks, to + ROWS * i:to + ROWS * (i + 1)]
                        counted(pool.tensor_copy(dst, src), "yc", s_yc)
                if i == 0:
                    for hl in range(2):
                        counted(pool.tensor_copy(ycol[:, b, hl, 0:LT, H + 4:H + 5], F(y[:, k, hl, 0:LT, PADC:PADC + 1])),
                                "yc", s_yc)
                        counted(pool.tensor_copy(ycol[0:LREM, b, hl, LT, H + 4:H + 5],
                                                 F(y[0:LREM, k, hl, LT, PADC:PADC + 1])), "yc", s_yc)

            counts = dict(hn=0, yc=0, pad0=0)

            def counted(ins, name, sm):
                counts[name] += 1
                ins.then_inc(sm, 1)
                pool.wait_ge(sm, counts[name])

            def deviation(b, i):
                rows = slice(64 + C * b, 64 + C * (b + 1))
                inverse_root(mv2[rows, :], mhalf[rows, :], s_var2[b], s_root2[b])

            handlers = {"scale": scale, "low": embed_padding, "norm": inverse_norms, "conva": embed_low, "split": query_low,
                        "deviation": deviation}
            first = before.index(("scale", 0, 1))
            perform(before[:first], handlers)
            tap_weights()
            perform(before[first:], handlers)
            first_padding(0)
            for s in range(steps):
                for n in range(3):
                    perform(gaps.get((s, n), []), handlers)
                if s >= NT:
                    continue
                g, j = s // TPC, s % TPC
                i = g % NCH
                if j == 0:
                    pool.wait_ge(s_el, s + 1)
                    if i:
                        row_behind(g - 1)
                    elif g:
                        first_padding(g)
                        last_padding(g - 1)
                if j == 2:
                    pool.wait_ge(s_el, s + 1)
                    pool.wait_ge(s_rl, 2 * (g + 1))
                    if i:
                        row_behind_last(g - 1)
                    column(g)
                if s == NT - 1:
                    last_padding(NG - 1)
            perform(behind, handlers)

        @block.tensor
        def _(pe):
            def misc(name, b, i):
                n = misc_no[name, b, i]
                if n >= 2:
                    wait_emptied(pe, *plan[n - 2])
                return pm[:, n % 2, :]

            def conv2(b, i):
                if b == 0:
                    pe.wait_ge(s_wst, 1)
                pe.wait_ge(s_x3[b], i + 1)
                o = misc("conv2", b, i)
                for n in range(4):
                    last = nc.tensor.matmul(o[0:96, 0:HALF], wst[:, P_W2:P_W2 + 96],
                                            x3v[:, HL // 2 * i:HL // 2 * (i + 1), n // 2, :, n % 2],
                                            start=n == 0, stop=n == 3)
                last.then_inc(s_mf, 1)

            def conv(name, at, b, i):
                o = misc(name, b, i)
                nc.tensor.matmul(o[0:96, 0:CHUNK], wst[:, at:at + 96], x3[:, CHUNK * i:CHUNK * (i + 1)],
                                 start=True, stop=True).then_inc(s_mf, 1)

            def norm(b, _):
                pe.wait_ge(s_sqs[b], 1)
                pe.wait_ge(s_const, 2)
                o = misc("norm", b, 0)
                for n in range(6):
                    cols = slice(96 * n, 96 * (n + 1))
                    last = nc.tensor.matmul(o[0:96, n:n + 1], sq[:, cols], ones[:, 0:1], start=True, stop=True)
                last.then_inc(s_mf, 1)

            def inverse_norms(b, i):
                pe.wait_ge(s_inv[b], 1)
                o = misc("inorm", b, i)
                for n in range(3):
                    last = nc.tensor.matmul(o[:, 96 * n:96 * (n + 1)],
                                            nrm[:, 6 + 3 * i + n:7 + 3 * i + n].to_broadcast([96, 128]), ident[0:96, 0:96],
                                            start=True, stop=True)
                last.then_inc(s_mf, 1)

            def tap_sums(b, n):
                column, beta, half = n // 4, n // 2 % 2, n % 2
                last_row = 2 * (MY // 2 * (half + 1) - 1) + 1 - 2
                pe.wait_ge(s_ef, NCH * b + min(last_row // ROWS + 1, NCH))
                pe.wait_ge(s_epad[b], 3)
                pe.wait_ge(s_ww, 4)
                o = misc("u", b, n)
                m = C if column else 128
                terms = [(a, kx) for a in ((1, 2) if beta else (0,)) for kx in ((1,) if column else range(6))]
                for k, (a, kx) in enumerate(terms):
                    r = MY * half + (1, 0, 1)[a]
                    lhs = ww[:, a, 5, 0:C] if column else ww[:, a, kx, :]
                    last = nc.tensor.matmul(o[0:m, 0:VHALF], lhs, e3v[:, r:r + MY - 1:2, kx:kx + W - 1:2],
                                            start=k == 0, stop=k == len(terms) - 1)
                last.then_inc(s_mf, 1)

            def tap_blocks(name, b, n):
                pe.wait_ge(s_vf[b], 8)
                groups, src, pair, size = (K_GROUPS, v, vp, 128) if name == "k" else (KC_GROUPS, vc, vcp, C)
                o = misc(name, b, n)
                for k, idx in enumerate(groups[n]):
                    if idx < PAIR:
                        kind, off = TAP_SRC[idx // LT]
                        at = VROW * kind + off + 128 * (idx % LT)
                        blk = src[:, at:at + 128]
                    elif idx < TOP:
                        blk = pair[:, idx - PAIR, :]
                    else:
                        blk = src[:, 128 * (idx - TOP):128 * (idx - TOP) + 128]
                    last = nc.tensor.transpose(o[:, size * k:size * (k + 1)], blk, ident[0:size, 0:size])
                last.then_inc(s_mf, 1)

            def scores(t):
                g = t // TPC
                b, k = t // (NT // B), g % 2
                cols = slice(128 * (t % TPC), 128 * (t % TPC + 1))
                pe.wait_ge(s_split, g + 1)
                if t % (NT // B) == 0:
                    pe.wait_ge(s_w[b], 1)
                if t:
                    pe.wait_ge(s_ex, t)
                pairs = ((mh, wh), (mh, wl), (ml, wh), (mr, wr))
                for n, (m, w) in enumerate(pairs):
                    for i in range(2):
                        last = nc.tensor.matmul(ps[:, i, 0:HALF], m[:, k, cols], w[b][:, HALF * i:HALF * (i + 1)],
                                                start=n == 0, stop=n == 3)
                last.then_inc(s_sc, 1)

            def transpose(t):
                k, j = t % 2, t % TPC
                pe.wait_ge(s_pn, t + 1)
                if t:
                    pe.wait_ge(s_el, t)
                if j == 0 and t:
                    pe.wait_ge(s_rl, 2 * (t // TPC))
                for i in range(LT):
                    nc.tensor.transpose(pt[:, i, :], p[:, k, 128 * i:128 * (i + 1)], ident[:, :])
                nc.tensor.transpose(pr[:, 128 * j:128 * (j + 1)], p[:, k, 128 * LT:L], ident[:, :]).then_inc(s_tr, 1)

            def tap_list(g):
                b, k = g // NCH, g % 2
                found = []
                def add(idx, blk, off, width, rows=128):
                    kk = [t[b][0:rows, idx, :] for t in (kh, kl)]
                    yy = [y[0:rows, k, hl, blk, off:off + width] for hl in range(2)]
                    found.append((kk[0], yy[0], width))
                    found.append((kk[0], yy[1], width))
                    found.append((kk[1], yy[0], width))
                for di in range(NDJ):
                    if di == 2:
                        add(PAIR, LT, 0, CHUNK)
                        if g % NCH == 0:
                            for i in range(LT + 1):
                                add(TOP + i, i, PADC, W, 128 if i < LT else LREM)
                    for i in range(LT):
                        add(LT * di + i, i, W * di, CHUNK)
                add(PAIR + 1, LT, PADC, CHUNK)
                return found

            def main(g, part, half):
                b, i = g // NCH, g % NCH
                if part == 0 and half == 0:
                    if i == 0:
                        wait_emptied(pe, "kc", b, 2)
                        pe.wait_ge(s_pad0, 3 * (b + 1))
                    else:
                        pe.wait_ge(s_hp, 3 * (g - b))
                    pe.wait_ge(s_rl, 2 * (g + 1))
                    if g >= 2:
                        pe.wait_ge(s_fin, 4 * (g - 1))
                work = tap_list(g)
                at_behind, at_last_behind = len(work) - 3 * (LT + 1), len(work) - 3
                sixth = 2 * part + half
                for n in range(len(work) * sixth // 6, len(work) * (sixth + 1) // 6):
                    lhs, rhs, width = work[n]
                    if n == at_behind:
                        pe.wait_ge(s_hn, 2 * g + 1)
                    if n == at_last_behind:
                        pe.wait_ge(s_hn, 2 * (g + 1))
                    last = nc.tensor.matmul(pa[:, g % 2, 0:width], lhs, rhs, start=n == 0, stop=n == len(work) - 1)
                if sixth == 5:
                    last.then_inc(s_mn, 1)

            def column_off(b, _):
                pe.wait_ge(s_yc, column_copies(NCH * (b + 1) - 1))
                o = misc("cc", b, 0)
                work = []
                for idx in range(NK):
                    if idx < PAIR:
                        rows, blk, at, width = 128, idx % LT, idx // LT, H
                    elif idx < TOP:
                        rows, blk, at, width = 128, LT, 2 * (idx - PAIR), H
                    else:
                        rows, blk, at, width = (128 if idx - TOP < LT else LREM), idx - TOP, H + 4, 2
                    for kk, hl in ((kch, 0), (kch, 1), (kcl, 0)):
                        work.append((kk[b][0:rows, idx, :], ycol[0:rows, b, hl, blk, at:at + width], width))
                for n, (lhs, rhs, width) in enumerate(work):
                    last = nc.tensor.matmul(o[0:C, 0:width], lhs, rhs, start=n == 0, stop=n == len(work) - 1)
                last.then_inc(s_mf, 1)

            def x1_turned(b, i):
                part = slice(64 + C * b, 64 + C * (b + 1))
                pe.wait_ge(s_xd[b], i + 1)
                o = misc("zn", b, i)
                for k in range(16):
                    at = W * (16 * i + k)
                    last = nc.tensor.transpose(o[0:W, C * k:C * (k + 1)], xd[part, at:at + W], ident[part, part])
                last.then_inc(s_mf, 1)

            def cosine_w(b, i):
                pe.wait_ge(s_cos, 16)
                wait_emptied(pe, "zn", b, 2)
                o = misc("d1", b, i)
                for k in range(8):
                    c = 16 * i + 2 * k
                    last = nc.tensor.matmul(o[0:2 * H, W * k:W * (k + 1)], zn[:, c:c + 2, :].rearrange("w c h -> w (c h)"),
                                            cosm[0:W, 0:W], start=True, stop=True)
                last.then_inc(s_mf, 1)

            def cosine_h(b, i):
                pe.wait_ge(s_cosl, 1)
                wait_emptied(pe, "d1", b, i)
                o = misc("d2", b, i)
                cols = slice(CHUNK * i, CHUNK * (i + 1))
                for n, (lhs, rhs) in enumerate(((cosh, d1h), (cosh, d1l), (cosl, d1h))):
                    last = nc.tensor.matmul(o[0:2 * H, 0:CHUNK], lhs[:, :], rhs[:, cols], start=n == 0, stop=n == 2)
                last.then_inc(s_mf, 1)

            handlers = {"conv2": conv2, "conv1": lambda b, i: conv("conv1", P_W1, b, i),
                        "conva": lambda b, i: conv("conva", P_WA, b, i), "norm": norm, "inorm": inverse_norms, "u": tap_sums,
                        "k": lambda b, i: tap_blocks("k", b, i), "kc": lambda b, i: tap_blocks("kc", b, i),
                        "cc": column_off, "zn": x1_turned, "d1": cosine_w, "d2": cosine_h}
            perform(before, handlers)
            scores(0)
            for s in range(steps):
                if s + 1 < NT:
                    scores(s + 1)
                g, part = divmod(s - LAG, TPC)
                perform(gaps.get((s, 0), []), handlers)
                if s >= LAG:
                    main(g, part, 0)
                perform(gaps.get((s, 1), []), handlers)
                if s >= LAG:
                    main(g, part, 1)
                perform(gaps.get((s, 2), []), handlers)
                if s < NT:
                    transpose(s)
            perform(behind, handlers)

        @block.scalar
        def _(act):
            def x_high(b, i):
                act.wait_ge(s_xn[b], i + 1)
                if b and i == 0:
                    act.wait_ge(s_mf, misc_no["conva", b - 1, NCH - 1] + 1)
                cols = slice(Q // 2 * i, Q // 2 * (i + 1))
                nc.scalar.activation(x3[:, cols], xn[:, cols], ACT.Copy).then_inc(s_x3h[b], 1)

            def residual(b, _):
                act.wait_ge(s_xin[b], 16)
                act.wait_ge(s_bd6, 1)
                part = slice(64 + C * b, 64 + C * (b + 1))
                nc.scalar.activation(v2[part, :], v2[part, :], ACT.Identity, bias=bd6[part, 0:1]).then_inc(s_xres[b], 1)

            def conv_sums(name, b, i, width, which, scale=1.0):
                o = group(act, name, b, i)
                k = conv_no(name, b, i)
                if k == 0:
                    act.wait_ge(s_nb, 2)
                if k >= 2:
                    act.wait_ge(s_zf, k - 1)
                if k >= ZBUF and embed_splits(k - ZBUF):
                    act.wait_ge(s_ef, embed_splits(k - ZBUF))
                nc.scalar.activation(zneg[:, k % 2, 0:width], o[0:96, 0:width], ACT.Relu, bias=nbias[:, which:which + 1],
                                     scale=-scale)
                nc.scalar.activation(z[:, k % ZBUF, 0:width], o[0:96, 0:width], ACT.Relu,
                                     bias=par[0:96, P_B1 + which:P_B1 + which + 1], scale=scale).then_inc(s_free["act"], 1)

            def query_high(b, i):
                g = NCH * b + i
                k, cols = g % 2, slice(CHUNK * i, CHUNK * (i + 1))
                if i == 0:
                    act.wait_ge(s_mim[b], 16 * IM2COL)
                if g >= 2:
                    act.wait_ge(s_sc, TPC * (g - 1))
                nc.scalar.activation(mh[:, k, :], vim[:, cols], ACT.Copy).then_inc(s_splith, 1)
                nc.scalar.activation(mr[:, k, :], v2[0:48, cols], ACT.Copy).then_inc(s_splith, 1)

            def squares(b, _):
                act.wait_ge(s_wim[b], 16 * IM2COL)
                nc.scalar.activation(sq[:, :], wim[:, :], ACT.Square).then_inc(s_sq[b], 1)
                nc.scalar.activation(sq8[:, :], wim8[0:CR, :], ACT.Square).then_inc(s_sq[b], 1)

            def keys_high(b, _):
                wait_emptied(act, "inorm", b, 1)
                nc.scalar.activation(wh[b][:, :], wim[:, :], ACT.Copy).then_inc(s_whi[b], 1)
                nc.scalar.activation(wr[b][:, :], wim8[:, :], ACT.Copy).then_inc(s_whi[b], 1)

            def tap_sums(b, n):
                if b and n == 0:
                    act.wait_ge(s_mf, misc_no["kc", b - 1, 2] + 1)
                o = group(act, "u", b, n)
                dst = vc if n // 4 else v
                at = VROW * (BETA if n // 2 % 2 else ALPHA) + VHALF * (n % 2)
                rows = C if n // 4 else 128
                nc.scalar.activation(dst[:, at:at + VHALF], o[0:rows, 0:VHALF], ACT.Copy).then_inc(s_free["act"], 1)

            def taps_high(name, b, n):
                if b and name == "k" and n == 0:
                    act.wait_ge(s_mim[b], 16 * IM2COL)
                groups, dst, size = (K_GROUPS, kh[b], 128) if name == "k" else (KC_GROUPS, kch[b], C)
                blocks = groups[n]
                o = group(act, name, b, n)
                nc.scalar.activation(dst[:, blocks[0]:blocks[-1] + 1, :], grouped(o, blocks, size), ACT.Copy,
                                     scale=-1.0 if blocks[0] >= TOP else 1.0).then_inc(s_kh, 1)

            def exp(t):
                act.wait_ge(s_mx, t + 1)
                if t >= 2:
                    act.wait_ge(s_tr, t - 1)
                nc.scalar.activation(p[:, t % 2, :].rearrange("p (a c) -> p a c", a=2), ps[:, :, 0:HALF], ACT.Exp,
                                     bias=negm[:, t % 2:t % 2 + 1], accum_out=psm[:, t % 2:t % 2 + 1]).then_inc(s_ex, 1)

            def softmax(t):
                k = t % 2
                act.wait_ge(s_rec, t + 1)
                nc.scalar.activation(p[:, k, :], p[:, k, :], ACT.Copy, scale=rps[:, k:k + 1]).then_inc(s_pn, 1)

            def y_high(t):
                g, j, k = t // TPC, t % TPC, t // TPC % 2
                act.wait_ge(s_tr, t + 1)
                if j == 0 and g >= 2:
                    act.wait_ge(s_mn, g - 1)
                    act.wait_ge(s_hp, 3 * (g - 1 - (g - 1) // NCH))
                    act.wait_ge(s_yc, column_copies(g - 2))
                at = PADC + 128 * j
                nc.scalar.activation(y[:, k, 0, 0:LT, at:at + 128], pt[:, :, :], ACT.Copy).then_inc(s_eh, 1)
                if j == TPC - 1:
                    nc.scalar.activation(y[0:LREM, k, 0, LT, PADC:PADC + CHUNK], pr[:, 0:CHUNK], ACT.Copy).then_inc(s_rh, 1)
                    nc.scalar.activation(y[LREM:128, k, 0, LT, W:W + CHUNK], pr[:, 0:CHUNK], ACT.Copy).then_inc(s_rh, 1)

            def rows_before(g):
                k, n = g % 2, (g - 1) % 2
                act.wait_ge(s_el, TPC * g)
                act.wait_ge(s_rl, 2 * g)
                if g >= 2:
                    act.wait_ge(s_mn, g - 1)
                for rows, blocks, width in ((slice(0, 128), slice(0, LT), PADC), (slice(0, LREM), LT, PADC),
                                            (slice(LREM, 128), LT, W)):
                    nc.scalar.activation(y[rows, k, :, blocks, 0:width], F(y[rows, n, :, blocks, CHUNK:CHUNK + width]),
                                         ACT.Copy).then_inc(s_hp, 1)

            def x1_turned(b, i):
                if i == 0:
                    if b:
                        act.wait_ge(s_mf, misc_no["d1", b - 1, 1] + 1)
                    else:
                        place_free(act)
                o = group(act, "zn", b, i)
                nc.scalar.activation(zn[:, :, 16 * i:16 * (i + 1)], o[0:W, 0:512].rearrange("w (h c) -> w c h", c=C),
                                     ACT.Copy).then_inc(s_free["act"], 1)

            def cosine_w(b, i):
                if b and i == 0:
                    act.wait_ge(s_mf, misc_no["d2", b - 1, 1] + 1)
                o = group(act, "d1", b, i)
                nc.scalar.activation(d1h[:, CHUNK * i:CHUNK * (i + 1)], o[0:2 * H, 0:CHUNK], ACT.Copy).then_inc(s_d1h, 1)

            handlers = {"scale": x_high, "residual": residual,
                        "conv2": lambda b, i: conv_sums("conv2", b, i, HALF, 1, 0.25),
                        "conv1": lambda b, i: conv_sums("conv1", b, i, CHUNK, 0),
                        "conva": lambda b, i: conv_sums("conva", b, i, CHUNK, 2),
                        "squares": squares, "keys": keys_high, "split": query_high, "u": tap_sums,
                        "k": lambda b, i: taps_high("k", b, i), "kc": lambda b, i: taps_high("kc", b, i),
                        "zn": x1_turned, "d1": cosine_w}
            perform(before, handlers)
            exp(0)
            for s in range(steps):
                if s < NT:
                    softmax(s)
                if s + 1 < NT:
                    exp(s + 1)
                if s < NT and s % TPC == 1 and s // TPC % NCH:
                    rows_before(s // TPC)
                for n in range(3):
                    perform(gaps.get((s, n), []), handlers)
                if s < NT:
                    y_high(s)
            perform(behind, handlers)

        @block.vector
        def _(dve):
            chain = [0]

            def link(ins):
                chain[0] += 1
                ins.then_inc(dve_chain, 1)
                dve.wait_ge(dve_chain, chain[0])

            def row_statistics(src, rows, stats, chunks):
                for i in chunks:
                    link(nc.vector.bn_stats(stats[rows, i, :], src[:, CHUNK * i:CHUNK * (i + 1)]))

            def variance(rows, stats, m, var_ready):
                link(nc.vector.bn_aggr(m[rows, 0:2], stats[rows, :, :]))
                nc.vector.tensor_scalar_add(m[rows, 1:2], m[rows, 1:2], GN_EPS).then_inc(var_ready, 1)

            def statistics(b, i):
                dve.wait_ge(s_x[b] if i else s_x0[b], 16 * 3)
                row_statistics(xn, slice(0, 96), bnst, (2 * i, 2 * i + 1))

            def scale(b, i):
                if i == 0:
                    variance(slice(0, 96), bnst, mv, s_var[b])
                    dve.wait_ge(s_root[b], 1)
                cols = slice(Q // 2 * i, Q // 2 * (i + 1))
                nc.vector.tensor_scalar(xn[:, cols], xn[:, cols], mv[:, 0:1], mv[:, 3:4], ALU.subtract,
                                        ALU.mult).then_inc(s_xn[b], 1)

            def x_low(b, i):
                cols = slice(Q // 2 * i, Q // 2 * (i + 1))
                dve.wait_ge(s_xn[b], i + 1)
                dve.wait_ge(s_x3h[b], i + 1)
                nc.vector.tensor_tensor(x3[64:96, cols], xn[64:96, cols], F(x3[64:96, cols]), ALU.subtract).then_inc(s_x3[b], 1)

            def conv_weights():
                dve.wait_ge(s_par, 16)
                nc.vector.tensor_scalar_mul(bd6[64:128, :], par[64:128, P_BD:P_BD + 1], 1.0 / 6.0).then_inc(s_bd6, 1)
                nc.vector.tensor_scalar_mul(nbias[:, :], par[0:96, P_B1:P_B1 + 3], -1.0).then_inc(s_nb, 1)
                nc.vector.tensor_scalar_mul(nslope[:, :], par[0:96, P_A1:P_A1 + 3], -1.0).then_inc(s_nb, 1)
                link(nc.vector.tensor_copy(wst[:, :], par[0:96, 0:P_WD]))
                nc.vector.tensor_tensor(wst[32:64, :], par[32:64, 0:P_WD], F(wst[32:64, :]), ALU.subtract).then_inc(s_wst, 1)

            def prelu(name, b, i, which, dst, width):
                k = conv_no(name, b, i)
                if k == 0:
                    dve.wait_ge(s_nb, 2)
                wait_emptied(dve, name, b, i)
                if name == "conva":
                    shaped = [t.rearrange("p (i j) -> p i j", j=W) for t in (zneg[:, k % 2, :], z[:, k % ZBUF, :])]
                    link(nc.vector.scalar_tensor_tensor(out=dst, in0=shaped[0], scalar=nslope[:, which:which + 1],
                                                        in1=shaped[1], op0=ALU.mult, op1=ALU.add))
                    nc.vector.scalar_tensor_tensor(out=z[64:96, k % ZBUF, :], in0=zneg[64:96, k % 2, :],
                                                   scalar=nslope[64:96, which:which + 1], in1=z[64:96, k % ZBUF, :],
                                                   op0=ALU.mult, op1=ALU.add).then_inc(s_zf, 1)
                else:
                    nc.vector.scalar_tensor_tensor(out=dst, in0=zneg[:, k % 2, 0:width], scalar=nslope[:, which:which + 1],
                                                   in1=z[:, k % ZBUF, 0:width], op0=ALU.mult, op1=ALU.add).then_inc(s_zf, 1)
                dve.wait_ge(s_zf, k + 1)

            def edges(image, row, size, ready):
                link(nc.vector.memset(image[32:64, 2 * row:2 * row + size:row], 0.0))
                nc.vector.memset(image[64:96, row + 1:row + 1 + size:row], 0.0).then_inc(ready, 1)

            def ref_image(b, i):
                if b and i == 0:
                    dve.wait_ge(s_wim[b - 1], 16 * IM2COL)
                prelu("conv2", b, i, 1, wimg[:, WL + 1 + HALF * i:WL + 1 + HALF * (i + 1)], HALF)
                if i == 1:
                    edges(wimg, WL, L, s_wimg[b])

            def match_image(b, i):
                if b and i == 0:
                    dve.wait_ge(s_mim[b - 1], 16 * IM2COL)
                prelu("conv1", b, i, 0, mimg[:, W + 1 + CHUNK * i:W + 1 + CHUNK * (i + 1)], CHUNK)
                if i == NCH - 1:
                    edges(mimg, W, Q, s_mimg[b])

            def embed(b, i):
                if i == 0:
                    dve.wait_ge(s_x3h[b], 2)
                prelu("conva", b, i, 2, e3v[:, 2 + ROWS * i:2 + ROWS * (i + 1), 2:2 + W], CHUNK)

            def squares_joined(b, _):
                dve.wait_ge(s_sq[b], 2)
                nc.vector.tensor_tensor(sq[0:CR, :], sq[0:CR, :], sq8[:, :], ALU.add).then_inc(s_sqs[b], 1)

            def norms(b, _):
                o = group(dve, "norm", b, 0)
                nc.vector.tensor_scalar_max(nrm[:, 0:6], o[0:96, 0:6], NORM_EPS ** 2).then_inc(s_free["dve"], 1)

            def keys_scaled(b, i):
                o = group(dve, "inorm", b, i)
                cols = slice(HALF * i, HALF * (i + 1))
                link(nc.vector.scalar_tensor_tensor(out=wim8[:, cols], in0=wim8[:, cols], scalar=SOFTMAX_SCALE,
                                                    in1=o[0:48, 0:HALF], op0=ALU.mult, op1=ALU.mult))
                nc.vector.scalar_tensor_tensor(out=wim[:, cols], in0=wim[:, cols], scalar=SOFTMAX_SCALE,
                                               in1=o[:, 0:HALF], op0=ALU.mult, op1=ALU.mult).then_inc(s_free["dve"], 1)

            def keys_low(b, _):
                wait_emptied(dve, "inorm", b, 1)
                dve.wait_ge(s_whi[b], 2)
                link(nc.vector.tensor_tensor(wl[b][:, :], wim[:, :], F(wh[b][:, :]), ALU.subtract))
                link(nc.vector.tensor_tensor(wr[b][0:32, :], wim8[0:32, :], F(wr[b][0:32, :]), ALU.subtract))
                nc.vector.tensor_copy(wr[b][0:CR, :], wim8[0:CR, :]).then_inc(s_w[b], 1)

            def tap_sums(b, n):
                wait_emptied(dve, "u", b, 7)
                src, pair = ((v, vp), (vc, vcp))[n]
                link(nc.vector.tensor_tensor(src[:, VROW * FULL:VROW * FULL + VROW - WL], src[:, 0:VROW - WL],
                                             src[:, VROW * BETA + WL:VROW * (BETA + 1)], ALU.add))
                for di in range(NDJ):
                    kind, off = TAP_SRC[di]
                    at = VROW * kind + off + 128 * LT
                    nc.vector.tensor_copy(pair[:, di // 2, LREM * (di % 2):LREM * (di % 2 + 1)],
                                          src[:, at:at + LREM]).then_inc(s_vf[b], 1)

            def taps_low(name, b, n):
                groups, high, low, size = (K_GROUPS, kh[b], kl[b], 128) if name == "k" else (KC_GROUPS, kch[b], kcl[b], C)
                blocks = groups[n]
                o = group(dve, name, b, n)
                dve.wait_ge(s_kh, 10 * b + n + 1 + (7 if name == "kc" else 0))
                cols = slice(blocks[0], blocks[-1] + 1)
                nc.vector.scalar_tensor_tensor(out=low[:, cols, :], in0=grouped(o, blocks, size),
                                               scalar=-1.0 if blocks[0] >= TOP else 1.0, in1=F(high[:, cols, :]),
                                               op0=ALU.mult, op1=ALU.subtract).then_inc(s_free["dve"], 1)

            def maximum(t):
                dve.wait_ge(s_sc, t + 1)
                nc.vector.tensor_reduce(negm[:, t % 2:t % 2 + 1], ps[:, :, 0:HALF], AX.XY, ALU.max,
                                        negate=True).then_inc(s_mx, 1)

            def inverse_sum(t):
                k = t % 2
                dve.wait_ge(s_ex, t + 1)
                nc.vector.reciprocal(rps[:, k:k + 1], psm[:, k:k + 1]).then_inc(s_rec, 1)

            def y_low(t):
                g, j, k = t // TPC, t % TPC, t // TPC % 2
                dve.wait_ge(s_eh, t + 1)
                at = PADC + 128 * j
                nc.vector.tensor_tensor(y[:, k, 1, 0:LT, at:at + 128], pt[:, :, :], F(y[:, k, 0, 0:LT, at:at + 128]),
                                        ALU.subtract).then_inc(s_el, 1)
                if j == TPC - 1:
                    dve.wait_ge(s_rh, 2 * (g + 1))
                    high = F(y[0:LREM, k, 0, LT, PADC:PADC + CHUNK])
                    nc.vector.tensor_tensor(y[0:LREM, k, 1, LT, PADC:PADC + CHUNK], pr[:, 0:CHUNK], high,
                                            ALU.subtract).then_inc(s_rl, 1)
                    nc.vector.tensor_tensor(y[LREM:128, k, 1, LT, W:W + CHUNK], pr[:, 0:CHUNK], high,
                                            ALU.subtract).then_inc(s_rl, 1)

            taps_read = [0]

            def finish(g, n):
                b, i = g // NCH, g % NCH
                if n == 0:
                    dve.wait_ge(s_mn, g + 1)
                    if i == 0:
                        dve.wait_ge(s_xres[b], 1)
                dj = (0, -2, -1, 1)[n]
                rows = x1(b)[:, CHUNK * i:CHUNK * (i + 1)].rearrange("c (i j) -> c i j", j=W)
                k = C * (dj + 2)
                acc = pa[k:k + C, g % 2, 0:CHUNK].rearrange("c (i j) -> c i j", j=W)
                lo, hi = max(0, -dj), W - max(0, dj)
                nc.vector.scalar_tensor_tensor(out=rows[:, :, lo:hi], in0=acc[:, :, lo + dj:hi + dj], scalar=1.0 / 6.0,
                                               in1=rows[:, :, lo:hi], op0=ALU.mult, op1=ALU.add).then_inc(s_fin, 1)
                dve.wait_ge(s_fin, 4 * g + n + 1)
                taps_read[0] += 1

            def column_off(b, _):
                assert taps_read[0] >= NDJ * NCH * b + 1
                o = group(dve, "cc", b, 0)
                col = x1(b)[:, 0:Q:W]
                nc.vector.scalar_tensor_tensor(out=col, in0=o[0:C, 0:H], scalar=-1.0 / 6.0, in1=col, op0=ALU.mult,
                                               op1=ALU.add).then_inc(s_free["dve"], 1)
                wait_emptied(dve, "cc", b, 0)

            def x1_rows(b):
                return slice(64 + C * b, 64 + C * (b + 1))

            def x1_statistics(b, i):
                assert taps_read[0] >= NDJ * (NCH * b + i + 1)
                row_statistics(x1(b), x1_rows(b), bnst2, (i,))

            def x1_deviation(b, _):
                assert taps_read[0] >= NDJ * NCH * (b + 1)
                row_statistics(x1(b), x1_rows(b), bnst2, (NCH - 1,))
                variance(x1_rows(b), bnst2, mv2, s_var2[b])

            def x1_normalise(b, i):
                if i == 0:
                    dve.wait_ge(s_root2[b], 1)
                    if b:
                        dve.wait_ge(s_mf, misc_no["zn", b - 1, 2] + 1)
                    else:
                        place_free(dve)
                rows, cols = x1_rows(b), slice(Q // 3 * i, Q // 3 * (i + 1))
                nc.vector.tensor_scalar(xd[rows, cols], x1(b)[:, cols], mv2[rows, 0:1], mv2[rows, 3:4], ALU.subtract,
                                        ALU.mult).then_inc(s_xd[b], 1)

            def cosine_w_low(b, i):
                o = group(dve, "d1", b, i)
                dve.wait_ge(s_d1h, 2 * b + i + 1)
                cols = slice(CHUNK * i, CHUNK * (i + 1))
                nc.vector.tensor_tensor(d1l[:, cols], o[0:2 * H, 0:CHUNK], F(d1h[:, cols]),
                                        ALU.subtract).then_inc(s_free["dve"], 1)

            def cosine_split(b, _):
                if b == 0:
                    dve.wait_ge(s_cos, 16)
                    link(nc.vector.tensor_copy(cosh[:, :], cosm[:, :]))
                    nc.vector.tensor_tensor(cosl[:, :], cosm[:, :], F(cosh[:, :]), ALU.subtract).then_inc(s_cosl, 1)

            def result(b, i):
                if i == 0:
                    dve.wait_ge(s_xr[b], 16 * 2)
                o = group(dve, "d2", b, i)
                cols = slice(CHUNK * i, CHUNK * (i + 1))
                nc.vector.tensor_tensor(res[b][:, cols], o[0:2 * H, 0:CHUNK], xr[b][:, cols],
                                        ALU.add).then_inc(s_free["dve"], 1)

            handlers = {"rows": statistics, "scale": scale, "low": x_low, "conv2": ref_image, "conv1": match_image,
                        "conva": embed, "squares": squares_joined, "norm": norms, "inorm": keys_scaled, "keys": keys_low,
                        "sums": tap_sums, "k": lambda b, i: taps_low("k", b, i), "kc": lambda b, i: taps_low("kc", b, i),
                        "cc": column_off, "stats": x1_statistics, "deviation": x1_deviation, "x1n": x1_normalise,
                        "residual": cosine_split, "d1": cosine_w_low, "d2": result}
            first = before.index(("low", 0, 0))
            perform(before[:first], handlers)
            conv_weights()
            perform(before[first:], handlers)
            maximum(0)
            inverse_sum(0)
            for s in range(steps):
                if s + 1 < NT:
                    maximum(s + 1)
                if 1 <= s <= NT:
                    y_low(s - 1)
                if s + 1 < NT:
                    inverse_sum(s + 1)
                for n in range(3):
                    g, tap = divmod(3 * (s - LAG - TPC) + n - FINISH_GAP, 3 * TPC)
                    if g >= 0 and tap < NDJ:
                        finish(g, tap)
                    perform(gaps.get((s, n), []), handlers)
            for n in range(NDJ):
                finish(NG - 1, n)
            perform(behind, handlers)


def kernel(**inputs):
    import concourse.bacc as bacc
    from concourse.bass_utils import run_bass_kernel_spmd

    a = {k.replace("L0_conv_", ""): np.asarray(v) for k, v in inputs.items()}
    par = np.zeros((128, NP), np.float32)
    w1t, w2t, wat = a["W1"].T, a["W2"].T, a["Wa"].T
    wdt = a["Wd"].transpose(1, 2, 3, 0).reshape(C, 9 * C)
    for r in range(3):
        rows = slice(32 * r, 32 * (r + 1))
        for k in range(3):
            par[rows, P_W1 + 32 * k:P_W1 + 32 * k + CR] = w1t
            par[rows, P_W2 + 32 * k:P_W2 + 32 * k + CR] = w2t
            par[rows, P_WA + 32 * k:P_WA + 32 * (k + 1)] = wat
        par[rows, P_WD:P_B1] = wdt
        par[32 * r:32 * r + CR, P_B1] = a["b1"]
        par[32 * r:32 * r + CR, P_B2] = a["b2"]
        par[rows, P_BA] = a["ba"]
    par[:, P_A1], par[:, P_A2], par[:, P_AA] = a["a1"][0], a["a2"][0], a["aa"][0]
    for b in range(B):
        par[64 + C * b:64 + C * (b + 1), P_BD] = a["bd"]
    k, n = np.arange(W)[:, None], np.arange(W)[None, :]
    dct = np.cos(np.pi * (2.0 * n + 1.0) * k / (2.0 * W)) * np.where(k == 0, np.sqrt(1.0 / W), np.sqrt(2.0 / W))
    arrays = {"x": np.ascontiguousarray(a["x"]), "params": par, "dct": np.kron(np.eye(2), dct.T).astype(np.float32)}

    nc = bacc.Bacc("TRN2", target_bir_lowering=False, num_devices=1)
    ins = [nc.dram_tensor(n, v.shape, F32, kind="ExternalInput").ap() for n, v in arrays.items()]
    out = nc.dram_tensor("out", (B, C, H, W), F32, kind="ExternalOutput").ap()
    x1_copy = nc.dram_tensor("x1_copy", (B, C, H * W), F32, kind="Internal").ap()
    program(nc, *ins, x1_copy, out)
    return run_bass_kernel_spmd(nc, [arrays], core_ids=[0]).results[0]["out"]
```
